# Optimizing a Trainium2 kernel written in Bass

```python
import numpy as np
import jax
import jax.numpy as jnp

def _softmax(x, axis=-1):
    return jax.nn.softmax(x, axis=axis)

def _gelu(x):
    return jax.nn.gelu(x, approximate=True)

def _silu(x):
    return jax.nn.silu(x)

def _sigmoid(x):
    return jax.nn.sigmoid(x)

def _layernorm(x, axis=-1, eps=1e-05):
    m = jnp.mean(x, axis=axis, keepdims=True)
    v = jnp.var(x, axis=axis, keepdims=True)
    return (x - m) / jnp.sqrt(v + eps)

def _scatter_add(tgt, idx, src, axis=0):
    return tgt.at[idx].add(src)

def _segment_sum(src, seg, n):
    return jax.ops.segment_sum(src, seg, n)
kernel_name = 'mk_flamingo_gated_d1_seqx_r2_a37bea'

def setup_inputs(seed: int=0):
    np.random.seed(seed)
    _w = jnp.asarray

    def _rec_inputs():
        import jax
        import jax.numpy as jnp
        _rk = jax.random.key(seed)
        x = -0.0003929 + 0.9999 * jax.random.normal(jax.random.fold_in(_rk, 1), (8, 1024, 512), jnp.float32)
        _lenS = 1024 - jax.random.randint(jax.random.fold_in(_rk, 7), (8,), 0, max(1, 1024 // 4) + 1, jnp.int32)
        _lenS2 = 1601 - jax.random.randint(jax.random.fold_in(_rk, 8), (8,), 0, max(1, 1601 // 4) + 1, jnp.int32)
        _ctx_1024P = jax.random.normal(jax.random.fold_in(_rk, 11), (8, 16, 512), jnp.float32)
        _ctx_1024c = jax.random.dirichlet(jax.random.fold_in(_rk, 511), 0.3 * jnp.ones((16,), jnp.float32), (8, 1601))
        _ctx_1024t = jnp.einsum('bsk,bkd->bsd', _ctx_1024c, _ctx_1024P)
        _ctx_1024t = _ctx_1024t * jax.lax.rsqrt(jnp.mean(jnp.square(_ctx_1024t)) + 1e-12) * 0.953939
        ctx_1024 = 2.81802e-05 + 1.00001 * (_ctx_1024t + 0.3 * jax.random.normal(jax.random.fold_in(_rk, 611), (8, 1601, 512), jnp.float32))
        _validS = jnp.arange(1024)[None, :] < _lenS[:, None]
        _validS2 = jnp.arange(1601)[None, :] < _lenS2[:, None]
        _causal = jnp.tril(jnp.ones((1024, 1024), dtype=bool))
        mask_SxS2_bk0 = jnp.logical_not(jnp.broadcast_to(_validS2[0:1, :], (1024, 1601)))
        _g = jax.random.normal(jax.random.fold_in(_rk, 9001), (2, 1), jnp.float32)
        _g = jnp.sign(_g) * jnp.maximum(jnp.abs(_g), 1.0) + (_g == 0) * 1.0
        g_xattn = _g[0]
        g_ffn = _g[1]
        return (x, ctx_1024, mask_SxS2_bk0, g_xattn, g_ffn)
    x, ctx_1024, mask_SxS2_bk0, g_xattn, g_ffn = _rec_inputs()

    def _L0_xattn_setup():
        import jax, jax.numpy as jnp
        import numpy as np
        B, S, D = (8, 1024, 512)
        key = jax.random.key(seed)
        ks = jax.random.split(key, 9)
        scale = 1.0 / np.sqrt(D)
        inp = {'query': jax.random.normal(ks[0], (B, S, D), dtype=jnp.float32), 'key': jax.random.normal(ks[1], (B, S, D), dtype=jnp.float32), 'value': jax.random.normal(ks[2], (B, S, D), dtype=jnp.float32), 'mask': jnp.tril(jnp.ones((S, S), dtype=bool)), 'Wq': jax.random.normal(ks[3], (D, D), dtype=jnp.float32) * scale, 'bq': jax.random.normal(ks[4], (D,), dtype=jnp.float32) * 0.02, 'Wk': jax.random.normal(ks[5], (D, D), dtype=jnp.float32) * scale, 'bk': jax.random.normal(ks[6], (D,), dtype=jnp.float32) * 0.02, 'Wv': jax.random.normal(ks[7], (D, D), dtype=jnp.float32) * scale, 'bv': jax.random.normal(ks[8], (D,), dtype=jnp.float32) * 0.02}
        return inp
    _L0_xattn_all = _L0_xattn_setup()
    _L0_xattn_in = {k: v for k, v in _L0_xattn_all.items() if k in ('Wq', 'bq', 'Wk', 'bk', 'Wv', 'bv')}
    del _L0_xattn_all

    def _L0_ffn_setup():
        import jax, jax.numpy as jnp
        import numpy as np
        CAPACITY_FACTOR = 0.5
        key = jax.random.key(seed)
        ks = jax.random.split(key, 5)
        B, S, D, F = (4, 2048, 512, 2048)
        scale_in = 1.0 / np.sqrt(D)
        scale_ff = 1.0 / np.sqrt(F)
        return {'hidden_states': jax.random.normal(ks[0], (B, S, D), dtype=jnp.float32), 'w_router': jax.random.normal(ks[1], (D,), dtype=jnp.float32) * scale_in, 'W1': jax.random.normal(ks[2], (D, F), dtype=jnp.float32) * scale_in, 'b1': jnp.zeros((F,), dtype=jnp.float32), 'W2': jax.random.normal(ks[3], (F, D), dtype=jnp.float32) * scale_ff, 'b2': jnp.zeros((D,), dtype=jnp.float32)}
    _L0_ffn_all = _L0_ffn_setup()
    _L0_ffn_in = {k: v for k, v in _L0_ffn_all.items() if k in ('w_router', 'W1', 'b1', 'W2', 'b2')}
    del _L0_ffn_all
    return {'x': x, 'ctx_1024': ctx_1024, 'mask_SxS2_bk0': mask_SxS2_bk0, 'g_xattn': g_xattn, 'g_ffn': g_ffn, 'L0_xattn_Wq': _L0_xattn_in['Wq'], 'L0_xattn_bq': _L0_xattn_in['bq'], 'L0_xattn_Wk': _L0_xattn_in['Wk'], 'L0_xattn_bk': _L0_xattn_in['bk'], 'L0_xattn_Wv': _L0_xattn_in['Wv'], 'L0_xattn_bv': _L0_xattn_in['bv'], 'L0_ffn_w_router': _L0_ffn_in['w_router'], 'L0_ffn_W1': _L0_ffn_in['W1'], 'L0_ffn_b1': _L0_ffn_in['b1'], 'L0_ffn_W2': _L0_ffn_in['W2'], 'L0_ffn_b2': _L0_ffn_in['b2']}

def reference(x, ctx_1024, mask_SxS2_bk0, g_xattn, g_ffn, L0_xattn_Wq, L0_xattn_bq, L0_xattn_Wk, L0_xattn_bk, L0_xattn_Wv, L0_xattn_bv, L0_ffn_w_router, L0_ffn_W1, L0_ffn_b1, L0_ffn_W2, L0_ffn_b2):
    import jax
    import jax.numpy as jnp

    def _L0_xattn_ref(query, key, value, mask, Wq, bq, Wk, bk, Wv, bv):
        import jax, jax.numpy as jnp
        import numpy as np
        B, S, D = (8, 1024, 512)
        dk = Wq.shape[1]
        q = jnp.einsum('bsd,de->bse', query, Wq) + bq
        k = jnp.einsum('bsd,de->bse', key, Wk) + bk
        v = jnp.einsum('bsd,de->bse', value, Wv) + bv
        scores = jnp.einsum('bqd,bkd->bqk', q, k) / jnp.sqrt(jnp.asarray(dk, q.dtype))
        scores = jnp.where(mask, scores, jnp.asarray(-jnp.inf, scores.dtype))
        attn = jax.nn.softmax(scores, axis=-1)
        return jnp.einsum('bqk,bkd->bqd', attn, v)

    def _L0_ffn_ref(hidden_states, w_router, W1, b1, W2, b2):
        import jax, jax.numpy as jnp
        import numpy as np
        CAPACITY_FACTOR = 0.5
        'Mixture-of-Depths block: route top-k tokens through an FFN inner block,\n            scatter back with sigmoid router weights; bypassed tokens pass through.'
        B, S, D = hidden_states.shape
        k = int(S * CAPACITY_FACTOR)
        scores = jnp.einsum('bsd,d->bs', hidden_states, w_router)
        top_scores, top_idx = jax.lax.top_k(scores, k)
        weights = jax.nn.sigmoid(top_scores)
        selected = jnp.take_along_axis(hidden_states, top_idx[:, :, None], axis=1)
        h = jax.nn.gelu(jnp.einsum('bkd,df->bkf', selected, W1) + b1)
        processed = jnp.einsum('bkf,fd->bkd', h, W2) + b2
        update = weights[:, :, None] * processed

        def scatter_one(xb, ib, ub):
            return xb.at[ib].add(ub)
        output = jax.vmap(scatter_one)(hidden_states, top_idx, update)
        return output
    x = x + jnp.tanh(g_xattn[0]) * _L0_xattn_ref(_layernorm(x, axis=-1), ctx_1024, ctx_1024, mask_SxS2_bk0, L0_xattn_Wq, L0_xattn_bq, L0_xattn_Wk, L0_xattn_bk, L0_xattn_Wv, L0_xattn_bv)
    x = x + jnp.tanh(g_ffn[0]) * _L0_ffn_ref(_layernorm(x, axis=-1), L0_ffn_w_router, L0_ffn_W1, L0_ffn_b1, L0_ffn_W2, L0_ffn_b2)
    return x

_drawn_inputs = setup_inputs


def setup_inputs(seed=0):
    import zlib

    import numpy as np

    out = dict(_drawn_inputs(seed))
    spreads = {'L0_ffn_b1': (0.0, 0.1), 'L0_ffn_b2': (0.0, 0.1)}
    factors = {'L0_xattn_bq': 2.977, 'L0_xattn_bk': 8.0, 'L0_xattn_bv': 4.069}
    for name, (base, spread) in spreads.items():
        noise = np.random.default_rng([zlib.crc32(name.encode()), seed]).standard_normal(out[name].shape)
        drawn = base * np.exp(spread * noise) if base else spread * noise
        out[name] = jnp.asarray(drawn.astype(out[name].dtype))
    for name, factor in factors.items():
        out[name] = (out[name] * factor).astype(out[name].dtype)
    return out
```

```python
from contextlib import ExitStack

import concourse.bass as bass
from concourse import mybir

F32 = mybir.dt.float32
F16 = mybir.dt.float16
U8 = mybir.dt.uint8
I32 = mybir.dt.int32
U32 = mybir.dt.uint32
ALU = mybir.AluOpType
ACT = mybir.ActivationFunctionType
AX = mybir.AxisListType

P = 128
BANK = 512
EPS = 1e-5

S_LN = 2.0 ** 2
S_A = 2.0 ** 4
S_W = 2.0 ** 8
S_Q = S_LN * S_A
S_CTX = 2.0 ** 4
S_P = 2.0 ** 12
S_OUT = 2.0 ** -2
S_G = 2.0 ** 6

MASKED = -3.0e38
FLOOR = -1.0e30
FAR = 1.0e6


class Bank:

    def __init__(self, index, n, per, split_n, split_per):
        self.index, self.n, self.per, self.split_n, self.split_per = index, n, per, split_n, split_per

    def use(self, batch):
        return batch * self.per + self.n

    def split(self, batch):
        return batch * self.split_per + self.split_n


def share_banks(steps, banks, is_split):
    uses = {b: 0 for b in banks}
    splits = {b: 0 for b in banks}
    dealt = []
    for k, step in enumerate(steps):
        b = banks[k % len(banks)]
        uses[b] += 1
        splits[b] += is_split(step)
        dealt.append((step, b, uses[b], splits[b]))
    return {step: Bank(b, n, uses[b], m, splits[b]) for step, b, n, m in dealt}


def wait_apart(eng, sem, value, passed):
    eng.wait_ge(sem, value)
    eng.sem_inc(passed, 1)


def flamingo_gated_layer(nc, x, ctx_in, mask, g_xattn, g_ffn, Wq, bq, Wk, bk, Wv, bv, w_router, W1, b1, W2, b2, out):
    B, S, D = x.shape
    K = ctx_in.shape[1]
    F = W1.shape[1]
    TOP = S // 2
    DC = D // P
    QT = S // P
    HALF = S // 2
    KB = (K + P - 1) // P
    TAIL = KB - 1
    TW = K - TAIL * P
    CB = 3
    NCH = TAIL // CB
    CW = CB * P
    FT = F // P
    ST = TOP // P
    assert TAIL % CB == 0 and D == BANK and TOP == BANK and CW <= BANK
    K_EXP = 1.0 / (D ** 0.5) / (S_Q * S_CTX)

    h2_rows = nc.dram_tensor("h2_rows", [B * S, D], F32, kind="Internal").ap()
    slot_table = nc.dram_tensor("slot_table", [B * TOP, 2], F32, kind="Internal").ap()
    out_rows = out.rearrange("b s d -> (b s) d")

    with ExitStack() as whole:
        def keep(name, shape, dt):
            return whole.enter_context(nc.sbuf_tensor(name, shape, dt))

        def sem(name):
            return whole.enter_context(nc.semaphore(name))

        ps = [whole.enter_context(nc.psum_tensor(f"bank{k}", [P, BANK], F32)) for k in range(8)]
        ident = keep("ident", [P, P], F32)
        unseen = keep("unseen", [P, QT, K], U8)
        a_hi = keep("a_hi", [P, DC, D], F16)
        a_lo = keep("a_lo", [P, DC, D], F16)
        wv_hi = keep("wv_hi", [P, DC, D], F16)
        wv_lo = keep("wv_lo", [P, DC, D], F16)
        q_bias = keep("q_bias", [P, DC], F32)
        r_hi = keep("r_hi", [P, DC], F16)
        r_lo = keep("r_lo", [P, DC], F16)
        r_bias = keep("r_bias", [P, 1], F32)
        tanh_x = keep("tanh_x", [P, 1], F32)
        tanh_f = keep("tanh_f", [P, 1], F32)
        bv_row = keep("bv_row", [P, D], F32)
        router_row = keep("router_row", [P, D], F32)
        minus_half = keep("minus_half", [P, 1], F32)
        seen_flags = keep("seen_flags", [1, NCH], I32)
        router = keep("router", [P, B * QT], F32)

        waits_passed = sem("waits_passed")

        with ExitStack() as part:
            def sb(name, shape, dt):
                return part.enter_context(nc.sbuf_tensor(name, shape, dt))

            wq_in = sb("wq_in", [P, DC, D], F32)
            wk_in = sb("wk_in", [P, DC, D], F32)
            wv_in = sb("wv_in", [P, DC, D], F32)
            wqT = sb("wqT", [P, DC, D], F32)
            wkT = sb("wkT", [P, DC, D], F32)
            mask_in = sb("mask_in", [P, QT, K], U8)
            bq_col = sb("bq_col", [P, DC], F32)
            bk_col = sb("bk_col", [P, DC], F32)
            gx_col = sb("gx_col", [P, 1], F32)
            gf_col = sb("gf_col", [P, 1], F32)
            tanh_gx = sb("tanh_gx", [P, 1], F32)
            bv_in = sb("bv_in", [P, D], F32)
            seen_part = sb("seen_part", [P, NCH], F32)
            seen_any = sb("seen_any", [P, NCH], F32)
            ones = sb("ones", [P, P], F32)

            s_wqk = sem("setup_wqk_loaded")
            s_small = sem("setup_small_loaded")
            s_wv = sem("setup_wv_loaded")
            s_mask = sem("setup_mask_loaded")
            s_ones = sem("setup_ones")
            s_ident = sem("setup_ident")
            s_turned = sem("setup_turned")
            s_copied = sem("setup_copied")
            s_mm = sem("setup_products")
            s_hi = sem("setup_hi")
            s_lo = sem("setup_lo")
            s_tanh = sem("setup_tanh")
            s_part = sem("setup_seen_part")
            s_any = sem("setup_seen_any")
            s_const = sem("setup_const")

            with nc.Block() as block:
                @block.sync
                def _(sp):
                    sp.dma_start(wq_in[:], Wq.rearrange("(c p) e -> p c e", p=P)).then_inc(s_wqk, 16)
                    sp.dma_start(wk_in[:], Wk.rearrange("(c p) e -> p c e", p=P)).then_inc(s_wqk, 16)
                    sp.dma_start(mask_in[:], mask.rearrange("(t p) k -> p t k", p=P)).then_inc(s_mask, 16)
                    sp.dma_start(wv_in[:], Wv.rearrange("(c p) e -> p c e", p=P)).then_inc(s_wv, 16)

                @block.gpsimd
                def _(pool):
                    nc.gpsimd.memset(ones[:], 1.0).then_inc(s_ones, 1)
                    pool.wait_ge(s_ones, 1)
                    nc.gpsimd.affine_select(out=ident[:], in_=ones[:], compare_op=ALU.is_equal, fill=0.0,
                                            base=0, pattern=[[-1, P]], channel_multiplier=1).then_inc(s_ident, 1)
                    nc.gpsimd.memset(minus_half[:], -0.5).then_inc(s_const, 1)
                    pool.wait_ge(s_part, NCH)
                    nc.gpsimd.partition_all_reduce(seen_any[:], seen_part[:], P,
                                                   bass.bass_isa.ReduceOp.max).then_inc(s_any, 1)

                @block.scalar
                def _(act):
                    with nc.allow_non_contiguous_dma(reason="a few hundred bias values, once"):
                        act.dma_start(bq_col[:], bq.rearrange("(c p) -> p c", p=P)).then_inc(s_small, 16)
                        act.dma_start(bk_col[:], bk.rearrange("(c p) -> p c", p=P)).then_inc(s_small, 16)
                    act.dma_start(gx_col[:], g_xattn.partition_broadcast(P)).then_inc(s_small, 16)
                    act.dma_start(gf_col[:], g_ffn.partition_broadcast(P)).then_inc(s_small, 16)
                    act.dma_start(bv_in[:], bv.partition_broadcast(P)).then_inc(s_small, 16)
                    act.dma_start(router_row[:], w_router.partition_broadcast(P)).then_inc(s_small, 16)
                    act.wait_ge(s_small, 96)
                    nc.scalar.activation(tanh_gx[:], gx_col[:], ACT.Tanh).then_inc(s_tanh, 1)
                    nc.scalar.activation(tanh_f[:], gf_col[:], ACT.Tanh).then_inc(s_tanh, 1)
                    act.wait_ge(s_wv, 16)
                    nc.scalar.activation(wv_hi[:], wv_in[:], ACT.Copy, scale=S_W).then_inc(s_hi, 1)
                    for c in range(DC):
                        act.wait_ge(s_mm, c + 1)
                        nc.scalar.activation(a_hi[:, c, :], ps[c][:], ACT.Copy, scale=S_A).then_inc(s_hi, 1)
                    act.wait_ge(s_mm, DC + 2)
                    nc.scalar.activation(r_hi[:], ps[5][:, 0:DC], ACT.Copy, scale=S_W).then_inc(s_hi, 1)
                    act.wait_ge(s_mask, 16)
                    nc.scalar.activation(unseen[:], mask_in[:], ACT.Copy, scale=-1.0, bias=1.0).then_inc(s_hi, 1)

                @block.tensor
                def _(pe):
                    pe.wait_ge(s_ident, 1)
                    pe.wait_ge(s_wqk, 32)
                    for n, w in enumerate((wq_in, wk_in)):
                        for f in range(DC):
                            for d in range(DC):
                                last = pe.transpose(ps[4 * n + f][:, d * P:(d + 1) * P],
                                                    w[:, d, f * P:(f + 1) * P], ident[:])
                            last.then_inc(s_turned, 1)
                    pe.wait_ge(s_copied, 2 * DC)
                    for d in range(DC):
                        for f in range(DC):
                            last = pe.matmul(ps[d][:], wqT[:, f, d * P:(d + 1) * P], wkT[:, f, :],
                                             start=(f == 0), stop=(f == DC - 1))
                        last.then_inc(s_mm, 1)
                    pe.wait_ge(s_small, 96)
                    for bank, w, col in ((4, wkT, bq_col), (5, wqT, bk_col)):
                        for d in range(DC):
                            for f in range(DC):
                                last = pe.matmul(ps[bank][:, d:d + 1], w[:, f, d * P:(d + 1) * P],
                                                 col[:, f:f + 1], start=(f == 0), stop=(f == DC - 1))
                        last.then_inc(s_mm, 1)
                    for f in range(DC):
                        last = pe.matmul(ps[6][:, 0:1], bq_col[:, f:f + 1].to_broadcast([P, P]),
                                         bk_col[:, f:f + 1], start=(f == 0), stop=(f == DC - 1))
                    last.then_inc(s_mm, 1)

                @block.vector
                def _(dve):
                    for n, w in enumerate((wqT, wkT)):
                        for f in range(DC):
                            dve.wait_ge(s_turned, DC * n + f + 1)
                            nc.vector.tensor_copy(w[:, f, :], ps[4 * n + f][:]).then_inc(s_copied, 1)
                    dve.wait_ge(s_mask, 16)
                    for c in range(NCH):
                        nc.vector.tensor_reduce(seen_part[:, c:c + 1], mask_in[:, :, c * CW:(c + 1) * CW],
                                                AX.XY, ALU.max).then_inc(s_part, 1)
                    dve.wait_ge(s_hi, 1)
                    nc.vector.scalar_tensor_tensor(out=wv_lo[:], in0=wv_in[:], scalar=S_W, in1=wv_hi[:],
                                                   op0=ALU.mult, op1=ALU.subtract).then_inc(s_lo, 1)
                    for c in range(DC):
                        dve.wait_ge(s_hi, c + 2)
                        nc.vector.scalar_tensor_tensor(out=a_lo[:, c, :], in0=ps[c][:], scalar=S_A,
                                                       in1=a_hi[:, c, :], op0=ALU.mult,
                                                       op1=ALU.subtract).then_inc(s_lo, 1)
                    dve.wait_ge(s_mm, DC + 1)
                    nc.vector.tensor_scalar(q_bias[:], ps[4][:, 0:DC], S_Q, None, ALU.mult).then_inc(s_lo, 1)
                    dve.wait_ge(s_hi, DC + 2)
                    nc.vector.scalar_tensor_tensor(out=r_lo[:], in0=ps[5][:, 0:DC], scalar=S_W, in1=r_hi[:],
                                                   op0=ALU.mult, op1=ALU.subtract).then_inc(s_lo, 1)
                    dve.wait_ge(s_mm, DC + 3)
                    nc.vector.tensor_scalar(r_bias[:], ps[6][:, 0:1], S_Q * S_CTX, None,
                                            ALU.mult).then_inc(s_lo, 1)
                    dve.wait_ge(s_tanh, 2)
                    nc.vector.tensor_scalar(tanh_x[:], tanh_gx[:], 1.0 / (S_OUT * S_W), None,
                                            ALU.mult).then_inc(s_lo, 1)
                    nc.vector.tensor_scalar(bv_row[:], bv_in[:], tanh_gx[:], None, ALU.mult).then_inc(s_lo, 1)
                    dve.wait_ge(s_any, 1)
                    nc.vector.tensor_copy(seen_flags[:], seen_any[0:1, :]).then_inc(s_lo, 1)

        with ExitStack() as part:
            def sb(name, shape, dt):
                return part.enter_context(nc.sbuf_tensor(name, shape, dt))

            def psem(name):
                return part.enter_context(nc.semaphore(name))

            x_in = [sb(f"x_in{s}", [P, D], F32) for s in range(2)]
            x_res = [sb(f"x_res{s}", [P, D], F32) for s in range(2)]
            h2 = [sb(f"h2_{s}", [P, D], F32) for s in range(2)]
            hT_hi = sb("hT_hi", [P, DC, S], F16)
            hT_lo = sb("hT_lo", [P, DC, S], F16)
            qT_hi = sb("qT_hi", [P, DC, S], F16)
            qT_lo = sb("qT_lo", [P, DC, S], F16)
            prob = [sb(f"prob{s}", [P, K], F32) for s in range(2)]
            pT_hi = sb("pT_hi", [P, KB, S], F16)
            pT_lo = sb("pT_lo", [P, KB, S], F16)
            c_in = [sb(f"c_in{s}", [P, D], F32) for s in range(4)]
            c_hi = sb("c_hi", [P, KB, D], F16)
            c_lo = sb("c_lo", [P, KB, D], F16)
            cT_hi = sb("cT_hi", [P, DC, K + 1], F16)
            cT_lo = sb("cT_lo", [P, DC, K + 1], F16)
            st1 = [sb(f"st1_{s}", [P, 6], F32) for s in range(2)]
            mv1 = [sb(f"mv1_{s}", [P, 2], F32) for s in range(2)]
            rs1 = [sb(f"rs1_{s}", [P, 1], F32) for s in range(2)]
            st2 = [sb(f"st2_{s}", [P, 6], F32) for s in range(2)]
            mv2 = [sb(f"mv2_{s}", [P, 2], F32) for s in range(2)]
            rs2 = [sb(f"rs2_{s}", [P, 1], F32) for s in range(2)]
            r_all = sb("r_all", [P, QT], F32)
            cmax = [sb(f"cmax{s}", [P, NCH + 1], F32) for s in range(2)]
            csum = [sb(f"csum{s}", [P, NCH + 1], F32) for s in range(2)]
            rmax = [sb(f"rmax_{s}", [P, 1], F32) for s in range(2)]
            smax = [sb(f"smax_{s}", [P, 1], F32) for s in range(2)]
            shift = [sb(f"shift{s}", [P, 1], F32) for s in range(2)]
            rsum = [sb(f"rsum_{s}", [P, 1], F32) for s in range(2)]
            rinv = [sb(f"rinv_{s}", [P, 1], F32) for s in range(2)]
            o_scale = sb("o_scale", [P, QT], F32)
            junk = [sb(f"junk{s}", [P, D], F16) for s in range(2)]
            router8 = sb("router8", [P, QT], F32)

            full = [psem(f"bank_full{k}") for k in range(8)]
            hi_out = [psem(f"bank_hi_out{k}") for k in range(8)]
            drained = [psem(f"bank_drained{k}") for k in range(8)]
            x_loaded = [psem(f"x_loaded{s}") for s in range(2)]
            xres_loaded = [psem(f"xres_loaded{s}") for s in range(2)]
            y_stored = [psem(f"y_stored{s}") for s in range(2)]
            h2_stored = [psem(f"h2_stored{s}") for s in range(2)]
            c_loaded = [psem(f"c_loaded{s}") for s in range(4)]
            c_used = [psem(f"c_used{s}") for s in range(4)]
            ln1_stats = psem("ln1_stats")
            ln1_moments = psem("ln1_moments")
            ln1_eps = psem("ln1_eps")
            ln1_rstd = psem("ln1_rstd")
            h_ready = psem("h_ready")
            chunk_max = psem("chunk_max")
            row_max = psem("row_max")
            held_max = psem("held_max")
            shift_ready = psem("shift_ready")
            probs_ready = psem("probs_ready")
            row_sum = psem("row_sum")
            row_inv = psem("row_inv")
            scale_ready = psem("scale_ready")
            xbias_ready = psem("xbias_ready")
            ln2_stats = psem("ln2_stats")
            ln2_moments = psem("ln2_moments")
            ln2_eps = psem("ln2_eps")
            ln2_rstd = psem("ln2_rstd")
            h2_ready = psem("h2_ready")
            y_ready = psem("y_ready")
            r_done = psem("router_tile_done")
            r_kept = psem("router_kept")
            presets = psem("presets")

            def early_first():
                steps = [("stats", 0), ("stats", 1)]
                for t in range(QT):
                    steps += [("norm", t), ("hT", t)]
                    if t + 2 < QT:
                        steps.append(("stats", t + 2))
                return steps + [("ctx", j) for j in range(KB)]

            def main_steps(prepare):
                e = prepare
                steps = [("Q", h, c) for h in range(2) for c in range(DC)] + [("R",)]
                for t in range(QT):
                    steps.append(("S", t))
                    if t > 0:
                        steps.append(("PT", t - 1))
                        if e:
                            steps += [("norm", t - 1), ("hT", t - 1)]
                    if e:
                        steps.append(("stats", t))
                steps += [("OT", 0, c) for c in range(DC)]
                if e:
                    steps += [("norm", QT - 1), ("hT", QT - 1)]
                steps.append(("PT", QT - 1))
                steps += [("O", 0)]
                for t in range(1, 4):
                    steps += [("O", t), ("Y", t - 1)]
                steps += [("OT", 1, c) for c in range(DC)]
                steps += [("Y", 3)]
                blocks = list(range(KB)) if e else []
                for t in range(4, QT):
                    steps += [("ctx", j) for j in blocks[:3]]
                    blocks = blocks[3:]
                    steps.append(("O", t))
                    if t > 4:
                        steps.append(("Y", t - 1))
                steps += [("ctx", j) for j in blocks] + [("Y", QT - 1)]
                return steps

            def groups_main():
                out_ = []
                for s in main_steps(False):
                    if s[0] in ("S", "PT"):
                        out_ += [s + (c,) for c in range(NCH + 1)]
                    elif s[0] in ("Q", "R", "OT", "O"):
                        out_.append(s)
                return out_

            at = share_banks(groups_main(), [0, 1, 2, 3, 4, 5], lambda s: s[0] in ("Q", "PT", "OT"))
            at.update(share_banks([s for s in early_first() if s[0] in ("hT", "ctx")], [6, 7],
                                  lambda s: True))
            c_uses = [len(range(s, KB, 4)) for s in range(4)]

            def turn(b, t):
                return b * QT + t + 1

            def is_drained(eng, step, b):
                g = at[step]
                eng.wait_ge(drained[g.index], g.use(b) + 1)

            def is_full(eng, step, b):
                g = at[step]
                eng.wait_ge(full[g.index], g.use(b))

            def is_free(eng, step, b):
                g = at[step]
                eng.wait_ge(drained[g.index], g.use(b))

            def hi_is_out(eng, step, b):
                g = at[step]
                eng.wait_ge(hi_out[g.index], g.split(b))

            def blocks_of(c):
                return range(c * CB, (c + 1) * CB) if c < NCH else range(TAIL, KB)

            def cols(c):
                return slice(c * CW, (c + 1) * CW) if c < NCH else slice(TAIL * P, K)

            def over_batches(eng, early, main):
                early(0)
                with eng.Fori(0, B - 1) as b:
                    main(b, main_steps(True))
                main(B - 1, main_steps(False))

            with nc.Block() as block:
                @block.sync
                def _(sp):
                    def load_x(b, t):
                        sp.dma_start(x_in[t % 2][:], x[bass.ds(b, 1), t * P:(t + 1) * P, :]
                                     .rearrange("o p d -> p (o d)")).then_inc(x_loaded[t % 2], 16)

                    def load_c(b, j):
                        rows = P if j < TAIL else TW
                        sp.dma_start(c_in[j % 4][0:rows, :], ctx_in[bass.ds(b, 1), j * P:j * P + rows, :]
                                     .rearrange("o p d -> p (o d)")).then_inc(c_loaded[j % 4], 16)

                    def load_xres(b, t):
                        sp.wait_ge(y_stored[t % 2], 16 * (QT // 2 * b + t // 2 + 1))
                        sp.dma_start(x_res[t % 2][:], x[bass.ds(b, 1), t * P:(t + 1) * P, :]
                                     .rearrange("o p d -> p (o d)")).then_inc(xres_loaded[t % 2], 16)

                    def early_step(b, s):
                        if s[0] == "hT" and s[1] + 2 < QT:
                            is_drained(sp, s, b)
                            load_x(b, s[1] + 2)
                        if s[0] == "ctx" and s[1] + 4 < KB:
                            j = s[1]
                            sp.wait_ge(c_used[j % 4], c_uses[j % 4] * b + j // 4 + 1)
                            load_c(b, j + 4)

                    def early(b):
                        for t in range(2):
                            load_x(b, t)
                        for j in range(4):
                            load_c(b, j)
                        for s in early_first():
                            early_step(b, s)

                    def main(b, steps):
                        prepare = ("ctx", 0) in steps
                        if prepare:
                            is_full(sp, ("Q", 0, 0), b)
                            for t in range(2):
                                load_x(b + 1, t)
                            for j in range(4):
                                sp.wait_ge(c_used[j], c_uses[j] * (b + 1))
                                load_c(b + 1, j)
                        load_xres(b, 0)
                        load_xres(b, 1)
                        for s in steps:
                            if s[0] in ("hT", "ctx"):
                                early_step(b + 1, s)
                            if s[0] == "Y":
                                t = s[1]
                                sp.wait_ge(h2_ready, turn(b, t))
                                sp.dma_start(h2_rows[bass.ds(b * S + t * P, P), :],
                                             h2[t % 2][:]).then_inc(h2_stored[t % 2], 16)
                                sp.wait_ge(y_ready, turn(b, t))
                                sp.dma_start(out_rows[bass.ds(b * S + t * P, P), :],
                                             x_res[t % 2][:]).then_inc(y_stored[t % 2], 16)
                                if t + 2 < QT:
                                    load_xres(b, t + 2)

                    over_batches(sp, early, main)
                    for s in range(2):
                        sp.wait_ge(y_stored[s], 16 * (QT // 2 * B + 1))
                        sp.wait_ge(h2_stored[s], 16 * (QT // 2 * B + 1))

                @block.gpsimd
                def _(pool):
                    for s in range(2):
                        nc.gpsimd.memset(cmax[s][:], MASKED).then_inc(presets, 1)
                        nc.gpsimd.memset(csum[s][:], 0.0).then_inc(presets, 1)
                        pool.sem_inc(y_stored[s], 16)
                        pool.sem_inc(h2_stored[s], 16)

                    def rstd(b, t, mv, rs, moments, eps_in, ready):
                        wait_apart(pool, moments, turn(b, t), waits_passed)
                        nc.gpsimd.tensor_scalar(rs[:], mv[:, 1:2], EPS, None, ALU.add).then_inc(eps_in, 1)
                        pool.wait_ge(eps_in, turn(b, t))
                        nc.gpsimd.tensor_tensor(rs[:], rs[:], minus_half[:], ALU.pow).then_inc(ready, 1)

                    def step(b, s):
                        if s[0] == "stats":
                            t = s[1]
                            rstd(b, t, mv1[t % 2], rs1[t % 2], ln1_moments, ln1_eps, ln1_rstd)

                    def early(b):
                        for s in early_first():
                            step(b, s)

                    def main(b, steps):
                        for s in steps:
                            if s[0] == "O":
                                t = s[1]
                                pool.wait_ge(xres_loaded[t % 2], 16 * (QT // 2 * b + t // 2 + 1))
                                nc.gpsimd.tensor_tensor(x_res[t % 2][:], x_res[t % 2][:], bv_row[:],
                                                        ALU.add).then_inc(xbias_ready, 1)
                                rstd(b, t, mv2[t % 2], rs2[t % 2], ln2_moments, ln2_eps, ln2_rstd)
                            else:
                                step(b + 1, s)

                    over_batches(pool, early, main)

                @block.tensor
                def _(pe):
                    seen = [pe.value_load(seen_flags[0:1, c:c + 1], min_val=0, max_val=1) for c in range(NCH)]

                    def products(dst, pairs, start=True, stop=True):
                        n = 3 * len(pairs)
                        k = 0
                        for sh, sl, mh, ml in pairs:
                            for st, mo in ((sh, mh), (sh, ml), (sl, mh)):
                                last = pe.matmul(dst, st, mo, start=start and k == 0,
                                                 stop=stop and k == n - 1, skip_group_check=True)
                                k += 1
                        return last

                    def Q(b, s):
                        _, h, c = s
                        g = at[s]
                        is_drained(pe, ("hT", 4 * h + 3), b)
                        is_free(pe, s, b)
                        e = slice(c * P, (c + 1) * P)
                        q = slice(h * HALF, (h + 1) * HALF)
                        products(ps[g.index][:], [(a_hi[:, d, e], a_lo[:, d, e], hT_hi[:, d, q], hT_lo[:, d, q])
                                                  for d in range(DC)]).then_inc(full[g.index], 1)

                    def R(b, s):
                        g = at[s]
                        is_free(pe, s, b)
                        for t in range(QT):
                            q = slice(t * P, (t + 1) * P)
                            last = products(ps[g.index][:, t:t + 1],
                                            [(hT_hi[:, d, q], hT_lo[:, d, q], r_hi[:, d:d + 1], r_lo[:, d:d + 1])
                                             for d in range(DC)])
                        last.then_inc(full[g.index], 1)

                    def scores(b, s, c):
                        t = s[1]
                        g = at[s + (c,)]
                        q = slice(t * P, (t + 1) * P)
                        return products(ps[g.index][:, 0:(CW if c < NCH else TW)],
                                        [(qT_hi[:, d, q], qT_lo[:, d, q], cT_hi[:, d, cols(c)], cT_lo[:, d, cols(c)])
                                         for d in range(DC)])

                    def S_(b, s):
                        t = s[1]
                        if t == 0:
                            pe.wait_ge(c_used[TAIL % 4], c_uses[TAIL % 4] * (b + 1))
                        if t % 4 == 0:
                            is_drained(pe, ("Q", t // 4, DC - 1), b)
                        for c in range(NCH):
                            g = at[s + (c,)]
                            is_free(pe, s + (c,), b)
                            with pe.If(seen[c] > 0):
                                scores(b, s, c).then_inc(full[g.index], 1)
                            with pe.Else():
                                pe.sem_inc(full[g.index], 1)
                        g = at[s + (NCH,)]
                        is_free(pe, s + (NCH,), b)
                        scores(b, s, NCH).then_inc(full[g.index], 1)

                    def turned(s, c):
                        t = s[1]
                        g = at[s + (c,)]
                        for k, j in enumerate(blocks_of(c)):
                            w = P if j < TAIL else TW
                            last = pe.transpose(ps[g.index][0:w, k * P:(k + 1) * P],
                                                prob[t % 2][:, j * P:j * P + w], ident[:])
                        return last

                    def PT(b, s):
                        pe.wait_ge(probs_ready, turn(b, s[1]))
                        for c in range(NCH):
                            g = at[s + (c,)]
                            is_free(pe, s + (c,), b)
                            with pe.If(seen[c] > 0):
                                turned(s, c).then_inc(full[g.index], 1)
                            with pe.Else():
                                pe.sem_inc(full[g.index], 1)
                        g = at[s + (NCH,)]
                        is_free(pe, s + (NCH,), b)
                        turned(s, NCH).then_inc(full[g.index], 1)

                    def OT(b, s):
                        _, h, c = s
                        g = at[s]
                        if c == 0:
                            is_drained(pe, ("PT", 4 * h + 3, NCH), b)
                        is_free(pe, s, b)
                        e = slice(c * P, (c + 1) * P)
                        q = slice(h * HALF, (h + 1) * HALF)
                        dst = ps[g.index][:]

                        def pair(j, w):
                            return c_hi[0:w, j, e], c_lo[0:w, j, e], pT_hi[0:w, j, q], pT_lo[0:w, j, q]

                        th, tl, ph, pl = pair(TAIL, TW)
                        pe.matmul(dst, th, ph, start=True, stop=False, skip_group_check=True)
                        for k in range(NCH):
                            with pe.If(seen[k] > 0):
                                products(dst, [pair(j, P) for j in blocks_of(k)], start=False, stop=False)
                        pe.matmul(dst, th, pl, start=False, stop=False, skip_group_check=True)
                        pe.matmul(dst, tl, ph, start=False, stop=True,
                                  skip_group_check=True).then_inc(full[g.index], 1)

                    def O(b, s):
                        t = s[1]
                        g = at[s]
                        if t % 4 == 0:
                            is_drained(pe, ("OT", t // 4, DC - 1), b)
                        is_free(pe, s, b)
                        q = slice(t * P, (t + 1) * P)
                        products(ps[g.index][:], [(qT_hi[:, d, q], qT_lo[:, d, q], wv_hi[:, d, :], wv_lo[:, d, :])
                                                  for d in range(DC)]).then_inc(full[g.index], 1)

                    def hT(b, s):
                        t = s[1]
                        g = at[s]
                        pe.wait_ge(h_ready, turn(b, t))
                        is_free(pe, s, b)
                        for d in range(DC):
                            last = pe.transpose(ps[g.index][:, d * P:(d + 1) * P],
                                                x_in[t % 2][:, d * P:(d + 1) * P], ident[:])
                        last.then_inc(full[g.index], 1)

                    def ctx_turned(s):
                        j = s[1]
                        g = at[s]
                        w = P if j < TAIL else TW
                        for d in range(DC):
                            last = pe.transpose(ps[g.index][:, d * P:d * P + w],
                                                c_in[j % 4][0:w, d * P:(d + 1) * P], ident[0:w, 0:w])
                        return last

                    def ctx(b, s):
                        j = s[1]
                        g = at[s]
                        pe.wait_ge(c_loaded[j % 4], 16 * (c_uses[j % 4] * b + j // 4 + 1))
                        is_free(pe, s, b)
                        if j == TAIL:
                            ctx_turned(s).then_inc(full[g.index], 1)
                        else:
                            with pe.If(seen[j // CB] > 0):
                                ctx_turned(s).then_inc(full[g.index], 1)
                            with pe.Else():
                                pe.sem_inc(full[g.index], 1)

                    does = {"Q": Q, "R": R, "S": S_, "PT": PT, "OT": OT, "O": O}
                    does_early = {"hT": hT, "ctx": ctx}

                    def early(b):
                        for s in early_first():
                            if s[0] in does_early:
                                does_early[s[0]](b, s)

                    def main(b, steps):
                        for s in steps:
                            if s[0] in does:
                                does[s[0]](b, s)
                            elif s[0] in does_early:
                                does_early[s[0]](b + 1, s)

                    over_batches(pe, early, main)

                @block.scalar
                def _(act):
                    seen = [act.value_load(seen_flags[0:1, c:c + 1], min_val=0, max_val=1) for c in range(NCH)]
                    act.wait_ge(presets, 4)

                    def Q(b, s):
                        _, h, c = s
                        g = at[s]
                        is_full(act, s, b)
                        nc.scalar.activation(qT_hi[:, c, h * HALF:(h + 1) * HALF], ps[g.index][:], ACT.Identity,
                                             bias=q_bias[:, c:c + 1]).then_inc(hi_out[g.index], 1)

                    def S_(b, s):
                        t = s[1]

                        def exp(c):
                            act.wait_ge(shift_ready, turn(b, t))
                            return nc.scalar.activation(prob[t % 2][:, cols(c)], prob[t % 2][:, cols(c)], ACT.Exp,
                                                        bias=shift[t % 2][:], scale=K_EXP,
                                                        accum_out=csum[t % 2][:, c:c + 1])
                        for c in range(NCH):
                            with act.If(seen[c] > 0):
                                exp(c)
                        exp(NCH).then_inc(probs_ready, 1)

                    def PT(b, s):
                        t = s[1]
                        q = slice(t * P, (t + 1) * P)
                        for c in range(NCH + 1):
                            g = at[s + (c,)]
                            if c < NCH:
                                with act.If(seen[c] > 0):
                                    is_full(act, s + (c,), b)
                                    nc.scalar.activation(pT_hi[:, c * CB:(c + 1) * CB, q],
                                                         ps[g.index][:, 0:CW].rearrange("p (j q) -> p j q", j=CB),
                                                         ACT.Copy, scale=S_P).then_inc(hi_out[g.index], 1)
                                with act.Else():
                                    is_full(act, s + (c,), b)
                                    act.sem_inc(hi_out[g.index], 1)
                            else:
                                is_full(act, s + (c,), b)
                                nc.scalar.activation(pT_hi[0:TW, TAIL, q], ps[g.index][0:TW, 0:P],
                                                     ACT.Copy, scale=S_P).then_inc(hi_out[g.index], 1)

                    def OT(b, s):
                        _, h, c = s
                        g = at[s]
                        is_full(act, s, b)
                        nc.scalar.activation(qT_hi[:, c, h * HALF:(h + 1) * HALF], ps[g.index][:], ACT.Copy,
                                             scale=S_OUT / (S_P * S_CTX)).then_inc(hi_out[g.index], 1)

                    def hT(b, s):
                        t = s[1]
                        g = at[s]
                        is_full(act, s, b)
                        nc.scalar.activation(hT_hi[:, :, t * P:(t + 1) * P],
                                             ps[g.index][:].rearrange("p (c q) -> p c q", c=DC),
                                             ACT.Copy, scale=S_LN).then_inc(hi_out[g.index], 1)

                    def ctx(b, s):
                        j = s[1]
                        g = at[s]
                        w = P if j < TAIL else TW

                        def arrived():
                            act.wait_ge(c_loaded[j % 4], 16 * (c_uses[j % 4] * b + j // 4 + 1))
                            is_full(act, s, b)

                        def split():
                            arrived()
                            nc.scalar.activation(cT_hi[:, :, j * P:j * P + w],
                                                 ps[g.index][:].rearrange("p (c k) -> p c k", c=DC)[:, :, 0:w],
                                                 ACT.Copy, scale=S_CTX)
                            nc.scalar.activation(c_hi[0:w, j, :], c_in[j % 4][0:w, :], ACT.Copy,
                                                 scale=S_CTX).then_inc(hi_out[g.index], 1)
                        if j == TAIL:
                            split()
                        else:
                            with act.If(seen[j // CB] > 0):
                                split()
                            with act.Else():
                                arrived()
                                act.sem_inc(hi_out[g.index], 1)

                    does = {"Q": Q, "S": S_, "PT": PT, "OT": OT}
                    does_early = {"hT": hT, "ctx": ctx}

                    def early(b):
                        for s in early_first():
                            if s[0] in does_early:
                                does_early[s[0]](b, s)

                    def main(b, steps):
                        for s in steps:
                            if s[0] in does:
                                does[s[0]](b, s)
                            elif s[0] in does_early:
                                does_early[s[0]](b + 1, s)

                    over_batches(act, early, main)

                @block.vector
                def _(dve):
                    seen = [dve.value_load(seen_flags[0:1, c:c + 1], min_val=0, max_val=1) for c in range(NCH)]
                    for k in range(8):
                        dve.sem_inc(drained[k], 1)
                    dve.wait_ge(presets, 4)

                    def lo_half(dst, src, scale, hi):
                        return nc.vector.scalar_tensor_tensor(out=dst, in0=src, scalar=scale, in1=hi,
                                                              op0=ALU.mult, op1=ALU.subtract)

                    def Q(b, s):
                        _, h, c = s
                        g = at[s]
                        q = slice(h * HALF, (h + 1) * HALF)
                        hi_is_out(dve, s, b)
                        nc.vector.scalar_tensor_tensor(out=qT_lo[:, c, q], in0=ps[g.index][:],
                                                       scalar=q_bias[:, c:c + 1], in1=qT_hi[:, c, q], op0=ALU.add,
                                                       op1=ALU.subtract).then_inc(drained[g.index], 1)

                    def R(b, s):
                        g = at[s]
                        is_full(dve, s, b)
                        nc.vector.tensor_scalar(r_all[:], ps[g.index][:, 0:QT], S_A * S_CTX / S_W, r_bias[:],
                                                ALU.mult, ALU.add).then_inc(drained[g.index], 1)

                    def S_(b, s):
                        t = s[1]

                        def masked(c, w):
                            g = at[s + (c,)]
                            return nc.vector.scalar_tensor_tensor(
                                out=prob[t % 2][:, cols(c)], in0=unseen[:, t, cols(c)], scalar=MASKED,
                                in1=ps[g.index][:, 0:w], op0=ALU.mult, op1=ALU.add)

                        for c in range(NCH):
                            g = at[s + (c,)]
                            with dve.If(seen[c] > 0):
                                is_full(dve, s + (c,), b)
                                masked(c, CW).then_inc(drained[g.index], 1)
                            with dve.Else():
                                is_full(dve, s + (c,), b)
                                dve.sem_inc(drained[g.index], 1)
                        g = at[s + (NCH,)]
                        is_full(dve, s + (NCH,), b)
                        masked(NCH, TW).then_inc(drained[g.index], 1)
                        for c in range(NCH):
                            with dve.If(seen[c] > 0):
                                is_drained(dve, s + (c,), b)
                                nc.vector.tensor_reduce(cmax[t % 2][:, c:c + 1], prob[t % 2][:, cols(c)],
                                                        AX.X, ALU.max)
                        is_drained(dve, s + (NCH,), b)
                        nc.vector.tensor_reduce(cmax[t % 2][:, NCH:NCH + 1], prob[t % 2][:, cols(NCH)],
                                                AX.X, ALU.max).then_inc(chunk_max, 1)
                        dve.wait_ge(chunk_max, turn(b, t))
                        nc.vector.tensor_reduce(rmax[t % 2][:], cmax[t % 2][:], AX.X, ALU.max).then_inc(row_max, 1)
                        dve.wait_ge(row_max, turn(b, t))
                        if t == 0:
                            is_drained(dve, ("R",), b)
                        nc.vector.tensor_scalar(smax[t % 2][:], rmax[t % 2][:], FLOOR, r_all[:, t:t + 1], ALU.max,
                                                ALU.add).then_inc(held_max, 1)
                        dve.wait_ge(held_max, turn(b, t))
                        nc.vector.tensor_scalar(shift[t % 2][:], smax[t % 2][:], r_all[:, t:t + 1], -K_EXP, ALU.subtract,
                                                ALU.mult).then_inc(shift_ready, 1)

                    def PT(b, s):
                        t = s[1]
                        q = slice(t * P, (t + 1) * P)
                        for c in range(NCH + 1):
                            g = at[s + (c,)]
                            if c < NCH:
                                with dve.If(seen[c] > 0):
                                    hi_is_out(dve, s + (c,), b)
                                    lo_half(pT_lo[:, c * CB:(c + 1) * CB, q],
                                            ps[g.index][:, 0:CW].rearrange("p (j q) -> p j q", j=CB), S_P,
                                            pT_hi[:, c * CB:(c + 1) * CB, q]).then_inc(drained[g.index], 1)
                                with dve.Else():
                                    hi_is_out(dve, s + (c,), b)
                                    dve.sem_inc(drained[g.index], 1)
                            else:
                                hi_is_out(dve, s + (c,), b)
                                lo_half(pT_lo[0:TW, TAIL, q], ps[g.index][0:TW, 0:P], S_P,
                                        pT_hi[0:TW, TAIL, q]).then_inc(drained[g.index], 1)
                        nc.vector.tensor_reduce(rsum[t % 2][:], csum[t % 2][:], AX.X, ALU.add).then_inc(row_sum, 1)
                        dve.wait_ge(row_sum, turn(b, t))
                        nc.vector.reciprocal(rinv[t % 2][:], rsum[t % 2][:]).then_inc(row_inv, 1)
                        dve.wait_ge(row_inv, turn(b, t))
                        nc.vector.tensor_scalar(o_scale[:, t:t + 1], rinv[t % 2][:], tanh_x[:], None,
                                                ALU.mult).then_inc(scale_ready, 1)

                    def OT(b, s):
                        _, h, c = s
                        g = at[s]
                        q = slice(h * HALF, (h + 1) * HALF)
                        hi_is_out(dve, s, b)
                        lo_half(qT_lo[:, c, q], ps[g.index][:], S_OUT / (S_P * S_CTX),
                                qT_hi[:, c, q]).then_inc(drained[g.index], 1)

                    def O(b, s):
                        t = s[1]
                        g = at[s]
                        xr = x_res[t % 2]
                        is_full(dve, s, b)
                        dve.wait_ge(xbias_ready, turn(b, t))
                        dve.wait_ge(scale_ready, turn(b, t))
                        nc.vector.scalar_tensor_tensor(out=xr[:], in0=ps[g.index][:], scalar=o_scale[:, t:t + 1],
                                                       in1=xr[:], op0=ALU.mult,
                                                       op1=ALU.add).then_inc(drained[g.index], 1)
                        is_drained(dve, s, b)
                        nc.vector.bn_stats(st2[t % 2][:], xr[:]).then_inc(ln2_stats, 1)
                        wait_apart(dve, ln2_stats, turn(b, t), waits_passed)
                        nc.vector.bn_aggr(mv2[t % 2][:], st2[t % 2][:]).then_inc(ln2_moments, 1)

                    def Y(b, s):
                        t = s[1]
                        xr = x_res[t % 2]
                        dve.wait_ge(ln2_rstd, turn(b, t))
                        dve.wait_ge(h2_stored[t % 2], 16 * (QT // 2 * b + t // 2 + 1))
                        nc.vector.tensor_scalar(h2[t % 2][:], xr[:], mv2[t % 2][:, 0:1], rs2[t % 2][:],
                                                ALU.subtract, ALU.mult).then_inc(h2_ready, 1)
                        dve.wait_ge(h2_ready, turn(b, t))
                        nc.vector.scalar_tensor_tensor(out=xr[:], in0=h2[t % 2][:], scalar=tanh_f[:], in1=xr[:],
                                                       op0=ALU.mult, op1=ALU.add).then_inc(y_ready, 1)
                        nc.vector.scalar_tensor_tensor(out=junk[t % 2][:], in0=h2[t % 2][:], scalar=1.0, in1=router_row[:],
                                                       op0=ALU.mult, op1=ALU.mult,
                                                       accum_out=router8[:, t:t + 1]).then_inc(r_done, 1)
                        if t == QT - 1:
                            dve.wait_ge(r_done, turn(b, t))
                            nc.vector.tensor_copy(router[:, bass.ds(b * QT, QT)], router8[:]).then_inc(r_kept, 1)

                    def stats(b, s):
                        t = s[1]
                        dve.wait_ge(x_loaded[t % 2], 16 * (QT // 2 * b + t // 2 + 1))
                        nc.vector.bn_stats(st1[t % 2][:], x_in[t % 2][:]).then_inc(ln1_stats, 1)
                        wait_apart(dve, ln1_stats, turn(b, t), waits_passed)
                        nc.vector.bn_aggr(mv1[t % 2][:], st1[t % 2][:]).then_inc(ln1_moments, 1)

                    def norm(b, s):
                        t = s[1]
                        dve.wait_ge(ln1_rstd, turn(b, t))
                        nc.vector.tensor_scalar(x_in[t % 2][:], x_in[t % 2][:], mv1[t % 2][:, 0:1], rs1[t % 2][:],
                                                ALU.subtract, ALU.mult).then_inc(h_ready, 1)

                    def hT(b, s):
                        t = s[1]
                        g = at[s]
                        q = slice(t * P, (t + 1) * P)
                        hi_is_out(dve, s, b)
                        lo_half(hT_lo[:, :, q], ps[g.index][:].rearrange("p (c q) -> p c q", c=DC), S_LN,
                                hT_hi[:, :, q]).then_inc(drained[g.index], 1)

                    def ctx(b, s):
                        j = s[1]
                        g = at[s]
                        w = P if j < TAIL else TW

                        def arrived():
                            dve.wait_ge(c_loaded[j % 4], 16 * (c_uses[j % 4] * b + j // 4 + 1))
                            hi_is_out(dve, s, b)

                        def split():
                            arrived()
                            lo_half(cT_lo[:, :, j * P:j * P + w],
                                    ps[g.index][:].rearrange("p (c k) -> p c k", c=DC)[:, :, 0:w], S_CTX,
                                    cT_hi[:, :, j * P:j * P + w]).then_inc(drained[g.index], 1)
                            lo_half(c_lo[0:w, j, :], c_in[j % 4][0:w, :], S_CTX,
                                    c_hi[0:w, j, :]).then_inc(c_used[j % 4], 1)
                        if j == TAIL:
                            split()
                        else:
                            with dve.If(seen[j // CB] > 0):
                                split()
                            with dve.Else():
                                arrived()
                                dve.sem_inc(drained[g.index], 1)
                                dve.sem_inc(c_used[j % 4], 1)

                    does = {"Q": Q, "R": R, "S": S_, "PT": PT, "OT": OT, "O": O, "Y": Y}
                    does_early = {"stats": stats, "norm": norm, "hT": hT, "ctx": ctx}

                    def early(b):
                        for s in early_first():
                            does_early[s[0]](b, s)

                    def main(b, steps):
                        for s in steps:
                            if s[0] in does:
                                does[s[0]](b, s)
                            else:
                                does_early[s[0]](b + 1, s)

                    over_batches(dve, early, main)

        with ExitStack() as part:
            def sb(name, shape, dt):
                return part.enter_context(nc.sbuf_tensor(name, shape, dt))

            def psem(name):
                return part.enter_context(nc.semaphore(name))

            NW1 = DC * (F // D)
            NW = NW1 + FT
            w_in = [sb(f"w_in{s}", [P, D], F32) for s in range(4)]
            w1_hi = sb("w1_hi", [P, DC, F], F16)
            w1_lo = sb("w1_lo", [P, DC, F], F16)
            w2_hi = sb("w2_hi", [P, FT, D], F16)
            w2_lo = sb("w2_lo", [P, FT, D], F16)
            b1_col = sb("b1_col", [P, FT], F32)
            b2_row = sb("b2_row", [P, D], F32)
            weight = sb("weight", [P, B * QT], F32)
            e_neg = sb("e_neg", [P, B * QT], F32)
            e_one = sb("e_one", [P, B * QT], F32)
            sig = sb("sig", [P, B * QT], F32)
            below = sb("below", [P, P], F32)
            tok_iota = sb("tok_iota", [P, QT], F32)
            slot_base = sb("slot_base", [P, 1], F32)
            row_base = sb("row_base", [P, 1], F32)
            r8 = sb("r8", [P, QT], F32)
            r_line = sb("r_line", [P, S], F32)
            cmp_junk = [sb(f"cmp_junk{s}", [P, S + P], F16) for s in range(2)]
            counts = sb("counts", [P, QT, 3], F32)
            rank = sb("rank", [P, QT], F32)
            far = sb("far", [P, QT], F32)
            slot_f = sb("slot_f", [P, QT], F32)
            slot = sb("slot", [P, QT], U32)
            entry = sb("entry", [P, QT, 2], F32)
            picked = sb("picked", [P, ST, 2], F32)
            row_next = sb("row_next", [P, ST], U32)
            row_now = sb("row_now", [P, ST], U32)
            weight_next = sb("weight_next", [P, ST], F32)
            weight_now = sb("weight_now", [P, ST], F32)
            sel = [sb(f"sel{s}", [P, D], F32) for s in range(ST)]
            selT_hi = sb("selT_hi", [P, DC, TOP], F16)
            selT_lo = sb("selT_lo", [P, DC, TOP], F16)
            act_f = [sb(f"act_f{s}", [P, TOP], F32) for s in range(2)]
            act_hi = [sb(f"act_hi{s}", [P, TOP], F16) for s in range(3)]
            act_lo = [sb(f"act_lo{s}", [P, TOP], F16) for s in range(3)]
            upd = [sb(f"upd{s}", [P, D], F32) for s in range(ST)]

            full = {k: psem(f"ffn_full{k}") for k in range(8)}
            hi_out = {k: psem(f"ffn_hi_out{k}") for k in range(8)}
            drained = {k: psem(f"ffn_drained{k}") for k in range(8)}
            w_loaded = [psem(f"w_loaded{s}") for s in range(4)]
            w_hi_done = psem("w_hi_done")
            w_lo_done = psem("w_lo_done")
            small_loaded = psem("small_loaded")
            const_ready = psem("const_ready")
            sig_step = psem("sig_step")
            weight_ready = psem("weight_ready")
            r8_ready = psem("r8_ready")
            counted = psem("counted")
            ranked = psem("ranked")
            far_ready = psem("far_ready")
            slotf_ready = psem("slotf_ready")
            entry_ready = psem("entry_ready")
            slots_ready = psem("slots_ready")
            table_written = psem("table_written")
            table_loaded = psem("table_loaded")
            rows_ready = psem("rows_ready")
            gathered = psem("gathered")
            act_hi_done = psem("act_hi_done")
            act_ready = psem("act_ready")
            upd_ready = psem("upd_ready")
            upd_added = psem("upd_added")
            adds_done = psem("adds_done")
            bases = psem("bases")

            def rank_steps():
                return [("line", 0), ("line", 1)] + [("rank", t) for t in range(QT)] + [("slots",)]

            def ffn_steps(prepare):
                steps = [("selT", s) for s in range(ST)]
                extra = {}
                if prepare:
                    extra = {1: [("line", 0), ("line", 1)], FT - 4: [("pick",)]}
                    for t in range(QT):
                        extra.setdefault(2 + t, []).append(("rank", t))
                    extra[1 + QT] = extra[1 + QT] + [("slots",)]
                for f in range(FT + 2):
                    if f < FT:
                        steps.append(("up", f))
                    if f == 0:
                        steps.append(("now",))
                    if f >= 2:
                        steps.append(("down", f - 2))
                    steps += extra.get(f, [])
                return steps + [("upd", s) for s in range(ST)]

            at = share_banks([s for s in ffn_steps(False) if s[0] in ("selT", "up")], [0, 1, 2],
                             lambda s: s[0] == "selT")
            at.update(share_banks([("line", 0), ("line", 1)], [7], lambda s: False))
            at.update({("upd", s): Bank(3 + s, 1, 1, 0, 0) for s in range(ST)})

            def is_drained(eng, step, b):
                g = at[step]
                eng.wait_ge(drained[g.index], g.use(b) + 1)

            def is_full(eng, step, b):
                g = at[step]
                eng.wait_ge(full[g.index], g.use(b))

            def is_free(eng, step, b):
                g = at[step]
                eng.wait_ge(drained[g.index], g.use(b))

            def hi_is_out(eng, step, b):
                g = at[step]
                eng.wait_ge(hi_out[g.index], g.split(b))

            def over_batches(eng, main):
                with eng.Fori(0, B - 1) as b:
                    main(b, ffn_steps(True))
                main(B - 1, ffn_steps(False))

            with nc.Block() as block:
                @block.sync
                def _(sp):
                    sp.dma_start(b2_row[:], b2.partition_broadcast(P)).then_inc(small_loaded, 16)
                    with nc.allow_non_contiguous_dma(reason="two thousand bias values, once"):
                        sp.dma_start(b1_col[:], b1.rearrange("(f p) -> p f", p=P)).then_inc(small_loaded, 16)
                    for n in range(NW):
                        if n < NW1:
                            src = W1[(n % DC) * P:(n % DC + 1) * P, (n // DC) * D:(n // DC + 1) * D]
                        else:
                            src = W2[(n - NW1) * P:(n - NW1 + 1) * P, :]
                        if n >= 4:
                            sp.wait_ge(w_lo_done, n - 3)
                        sp.dma_start(w_in[n % 4][:], src).then_inc(w_loaded[n % 4], 16)

                    def pick(b):
                        sp.wait_ge(table_written, 16 * QT * (b + 1))
                        sp.dma_start(picked[:], slot_table[bass.ds(b * TOP, TOP), :]
                                     .rearrange("(s p) c -> p s c", p=P)).then_inc(table_loaded, 16)

                    pick(0)
                    with sp.Fori(0, B - 1) as b:
                        pick(b + 1)

                @block.gpsimd
                def _(pool):
                    nc.gpsimd.memset(below[:], 1.0).then_inc(const_ready, 1)
                    pool.wait_ge(const_ready, 1)
                    nc.gpsimd.affine_select(out=below[:], in_=below[:], compare_op=ALU.is_ge, fill=0.0, base=-1,
                                            pattern=[[-1, P]], channel_multiplier=1).then_inc(const_ready, 1)
                    nc.gpsimd.iota(tok_iota[:], [[P, QT]], base=0, channel_multiplier=1,
                                   allow_small_or_imprecise_dtypes=True).then_inc(const_ready, 1)
                    nc.gpsimd.memset(slot_base[:], 0.0).then_inc(const_ready, 1)
                    nc.gpsimd.memset(row_base[:], 0.0).then_inc(const_ready, 1)
                    nc.gpsimd.memset(counts[:], 0.0).then_inc(const_ready, 1)
                    pool.sem_inc(adds_done, 1)

                    def fill_table(b):
                        wait_apart(pool, entry_ready, b + 1, waits_passed)
                        wait_apart(pool, slots_ready, b + 1, waits_passed)
                        for t in range(QT):
                            pool.indirect_dma_start(slot_table, bass.IndirectOffsetOnAxis(ap=slot[:, t:t + 1], axis=0),
                                                    entry[:, t, :], None, bounds_check=B * TOP - 1,
                                                    oob_is_err=False).then_inc(table_written, 16)

                    def gather(b):
                        wait_apart(pool, rows_ready, b + 1, waits_passed)
                        for s in range(ST):
                            pool.indirect_dma_start(sel[s][:], None, h2_rows,
                                                    bass.IndirectOffsetOnAxis(ap=row_next[:, s:s + 1], axis=0),
                                                    bounds_check=B * S - 1,
                                                    oob_is_err=True).then_inc(gathered, 16)

                    def main(b, steps):
                        for s in steps:
                            if s[0] == "slots":
                                fill_table(b + 1)
                            if s[0] == "pick":
                                gather(b + 1)
                            if s[0] == "upd":
                                k = s[1]
                                wait_apart(pool, upd_ready, ST * b + k + 1, waits_passed)
                                pool.indirect_dma_start(out_rows,
                                                        bass.IndirectOffsetOnAxis(ap=row_now[:, k:k + 1], axis=0),
                                                        upd[k][:], None, bounds_check=B * S - 1, oob_is_err=True,
                                                        compute_op=ALU.add).then_inc(upd_added, 16)
                        pool.wait_ge(upd_added, 16 * ST * (b + 1))
                        pool.sem_inc(adds_done, 1)

                    fill_table(0)
                    gather(0)
                    over_batches(pool, main)
                    pool.wait_ge(upd_added, 16 * ST * B)

                @block.tensor
                def _(pe):
                    def line(b, s):
                        g = at[s]
                        pe.wait_ge(r8_ready, b + 1)
                        is_free(pe, s, b)
                        for k in range(4):
                            t = 4 * s[1] + k
                            last = pe.transpose(ps[g.index][:, k * P:(k + 1) * P],
                                                r8[:, t:t + 1].to_broadcast([P, P]), ident[:])
                        last.then_inc(full[g.index], 1)

                    def selT(b, s):
                        k = s[1]
                        g = at[s]
                        if k == 0:
                            pe.wait_ge(gathered, 16 * ST * (b + 1))
                        is_free(pe, s, b)
                        for d in range(DC):
                            last = pe.transpose(ps[g.index][:, d * P:(d + 1) * P], sel[k][:, d * P:(d + 1) * P],
                                                ident[:])
                        last.then_inc(full[g.index], 1)

                    def up(b, s):
                        f = s[1]
                        g = at[s]
                        if f == 0:
                            is_drained(pe, ("selT", ST - 1), b)
                        is_free(pe, s, b)
                        fs = slice(f * P, (f + 1) * P)
                        for d in range(DC):
                            for k, (st, mo) in enumerate(((w1_hi, selT_hi), (w1_hi, selT_lo), (w1_lo, selT_hi))):
                                last = pe.matmul(ps[g.index][:], st[:, d, fs], mo[:, d, :],
                                                 start=(d == 0 and k == 0), stop=(d == DC - 1 and k == 2))
                        last.then_inc(full[g.index], 1)

                    def down(b, s):
                        f = s[1]
                        pe.wait_ge(act_ready, FT * b + f + 3)
                        for k in range(ST):
                            g = at[("upd", k)]
                            if f == 0:
                                is_free(pe, ("upd", k), b)
                            ts = slice(k * P, (k + 1) * P)
                            for n, (st, mo) in enumerate(((act_hi, w2_hi), (act_hi, w2_lo), (act_lo, w2_hi))):
                                last = pe.matmul(ps[g.index][:], st[f % 3][:, ts], mo[:, f, :],
                                                 start=(f == 0 and n == 0), stop=(f == FT - 1 and n == 2),
                                                 skip_group_check=True)
                            if f == FT - 1:
                                last.then_inc(full[g.index], 1)

                    def main(b, steps):
                        for s in steps:
                            if s[0] == "line":
                                line(b + 1, s)
                            elif s[0] in ("selT", "up", "down"):
                                {"selT": selT, "up": up, "down": down}[s[0]](b, s)

                    line(0, ("line", 0))
                    line(0, ("line", 1))
                    pe.wait_ge(w_lo_done, NW)
                    over_batches(pe, main)

                @block.scalar
                def _(act):
                    nc.scalar.activation(e_neg[:], router[:], ACT.Exp, scale=-1.0).then_inc(sig_step, 1)
                    for n in range(NW):
                        act.wait_ge(w_loaded[n % 4], 16 * (n // 4 + 1))
                        dst = w1_hi[:, n % DC, (n // DC) * D:(n // DC + 1) * D] if n < NW1 else w2_hi[:, n - NW1, :]
                        nc.scalar.activation(dst, w_in[n % 4][:], ACT.Copy, scale=S_W).then_inc(w_hi_done, 1)
                    act.wait_ge(small_loaded, 32)

                    def main(b, steps):
                        for s in steps:
                            if s[0] == "selT":
                                g = at[s]
                                is_full(act, s, b)
                                nc.scalar.activation(selT_hi[:, :, s[1] * P:(s[1] + 1) * P],
                                                     ps[g.index][:].rearrange("p (c q) -> p c q", c=DC),
                                                     ACT.Copy, scale=S_LN).then_inc(hi_out[g.index], 1)
                            if s[0] == "up":
                                f = s[1]
                                g = at[s]
                                is_full(act, s, b)
                                act.wait_ge(act_ready, FT * b + f + 1)
                                nc.scalar.activation(act_f[f % 2][:], ps[g.index][:], ACT.Gelu_apprx_tanh,
                                                     bias=b1_col[:, f:f + 1],
                                                     scale=1.0 / (S_LN * S_W)).then_inc(drained[g.index], 1)
                                is_drained(act, s, b)
                                nc.scalar.activation(act_hi[f % 3][:], act_f[f % 2][:], ACT.Copy,
                                                     scale=S_G).then_inc(act_hi_done, 1)

                    over_batches(act, main)

                @block.vector
                def _(dve):
                    for k in range(8):
                        dve.sem_inc(drained[k], 1)
                    dve.sem_inc(act_ready, 2)

                    def take_scores(b):
                        if not isinstance(b, int) or b > 0:
                            dve.wait_ge(table_written, 16 * QT * b)
                        nc.vector.tensor_copy(r8[:], router[:, bass.ds(b * QT, QT)]).then_inc(r8_ready, 1)
                        nc.vector.tensor_scalar(entry[:, :, 0], tok_iota[:], row_base[:], None,
                                                ALU.add)
                        nc.vector.tensor_copy(entry[:, :, 1], weight[:, bass.ds(b * QT, QT)]).then_inc(entry_ready, 1)
                        nc.vector.tensor_scalar(row_base[:], row_base[:], float(S), None, ALU.add).then_inc(bases, 1)

                    def line(b, s):
                        g = at[s]
                        is_full(dve, s, b)
                        nc.vector.tensor_copy(r_line[:, s[1] * BANK:(s[1] + 1) * BANK],
                                              ps[g.index][:]).then_inc(drained[g.index], 1)
                        is_drained(dve, s, b)

                    def rank_tile(b, s):
                        t = s[1]
                        me = r8[:, t:t + 1]
                        junk = cmp_junk[t % 2]
                        if t > 1:
                            dve.wait_ge(counted, QT * b + t - 1)
                        if t > 0:
                            nc.vector.tensor_scalar(junk[:, 0:t * P], r_line[:, 0:t * P], me, None, ALU.is_ge,
                                                    ALU.add, accum_out=counts[:, t, 0:1])
                        nc.vector.tensor_scalar(junk[:, t * P:S], r_line[:, t * P:S], me, None, ALU.is_gt,
                                                ALU.add, accum_out=counts[:, t, 1:2])
                        nc.vector.scalar_tensor_tensor(out=junk[:, S:S + P], in0=r_line[:, t * P:(t + 1) * P],
                                                       scalar=me, in1=below[:], op0=ALU.is_equal, op1=ALU.mult,
                                                       accum_out=counts[:, t, 2:3]).then_inc(counted, 1)

                    def slots(b):
                        dve.wait_ge(counted, QT * (b + 1))
                        nc.vector.tensor_reduce(rank[:], counts[:], AX.X, ALU.add).then_inc(ranked, 1)
                        dve.wait_ge(ranked, b + 1)
                        nc.vector.tensor_scalar(far[:], rank[:], float(TOP), FAR, ALU.is_ge,
                                                ALU.mult).then_inc(far_ready, 1)
                        dve.wait_ge(far_ready, b + 1)
                        nc.vector.scalar_tensor_tensor(out=slot_f[:], in0=rank[:], scalar=slot_base[:], in1=far[:],
                                                       op0=ALU.add, op1=ALU.add).then_inc(slotf_ready, 1)
                        dve.wait_ge(slotf_ready, b + 1)
                        nc.vector.tensor_copy(slot[:], slot_f[:]).then_inc(slots_ready, 1)
                        nc.vector.tensor_scalar(slot_base[:], slot_base[:], float(TOP), None,
                                                ALU.add).then_inc(bases, 1)

                    def pick(b):
                        dve.wait_ge(table_loaded, 16 * (b + 1))
                        nc.vector.tensor_copy(weight_next[:], picked[:, :, 1])
                        nc.vector.tensor_copy(row_next[:], picked[:, :, 0]).then_inc(rows_ready, 1)

                    dve.wait_ge(const_ready, 6)
                    dve.wait_ge(sig_step, 1)
                    nc.vector.tensor_scalar(e_one[:], e_neg[:], 1.0, None, ALU.add).then_inc(sig_step, 1)
                    dve.wait_ge(sig_step, 2)
                    nc.vector.reciprocal(sig[:], e_one[:]).then_inc(sig_step, 1)
                    dve.wait_ge(sig_step, 3)
                    nc.vector.tensor_scalar(weight[:], sig[:], tanh_f[:], None, ALU.mult).then_inc(weight_ready, 1)
                    dve.wait_ge(weight_ready, 1)
                    take_scores(0)
                    for s in rank_steps():
                        if s[0] == "line":
                            line(0, s)
                        elif s[0] == "rank":
                            rank_tile(0, s)
                        else:
                            slots(0)
                    for n in range(NW):
                        dve.wait_ge(w_hi_done, n + 1)
                        if n < NW1:
                            c, q = n % DC, slice((n // DC) * D, (n // DC + 1) * D)
                            lo, hi = w1_lo[:, c, q], w1_hi[:, c, q]
                        else:
                            lo, hi = w2_lo[:, n - NW1, :], w2_hi[:, n - NW1, :]
                        nc.vector.scalar_tensor_tensor(out=lo, in0=w_in[n % 4][:], scalar=S_W, in1=hi, op0=ALU.mult,
                                                       op1=ALU.subtract).then_inc(w_lo_done, 1)
                    pick(0)
                    dve.wait_ge(small_loaded, 32)

                    def main(b, steps):
                        for s in steps:
                            if s[0] == "selT":
                                g = at[s]
                                q = slice(s[1] * P, (s[1] + 1) * P)
                                hi_is_out(dve, s, b)
                                nc.vector.scalar_tensor_tensor(
                                    out=selT_lo[:, :, q], in0=ps[g.index][:].rearrange("p (c q) -> p c q", c=DC),
                                    scalar=S_LN, in1=selT_hi[:, :, q], op0=ALU.mult,
                                    op1=ALU.subtract).then_inc(drained[g.index], 1)
                            elif s[0] == "now":
                                dve.wait_ge(adds_done, b + 1)
                                nc.vector.tensor_copy(row_now[:], row_next[:])
                                nc.vector.tensor_copy(weight_now[:], weight_next[:])
                                if ("line", 0) in steps:
                                    take_scores(b + 1)
                            elif s[0] == "up":
                                f = s[1]
                                dve.wait_ge(act_hi_done, FT * b + f + 1)
                                nc.vector.scalar_tensor_tensor(out=act_lo[f % 3][:], in0=act_f[f % 2][:], scalar=S_G,
                                                               in1=act_hi[f % 3][:], op0=ALU.mult,
                                                               op1=ALU.subtract).then_inc(act_ready, 1)
                            elif s[0] == "line":
                                line(b + 1, s)
                            elif s[0] == "rank":
                                rank_tile(b + 1, s)
                            elif s[0] == "slots":
                                slots(b + 1)
                            elif s[0] == "pick":
                                pick(b + 1)
                            elif s[0] == "upd":
                                k = s[1]
                                g = at[s]
                                is_full(dve, s, b)
                                nc.vector.scalar_tensor_tensor(out=upd[k][:], in0=ps[g.index][:],
                                                               scalar=1.0 / (S_G * S_W), in1=b2_row[:], op0=ALU.mult,
                                                               op1=ALU.add).then_inc(drained[g.index], 1)
                                is_drained(dve, s, b)
                                nc.vector.tensor_scalar(upd[k][:], upd[k][:], weight_now[:, k:k + 1], None,
                                                        ALU.mult).then_inc(upd_ready, 1)

                    over_batches(dve, main)


_INS = ['x', 'ctx_1024', 'mask_SxS2_bk0', 'g_xattn', 'g_ffn', 'L0_xattn_Wq', 'L0_xattn_bq', 'L0_xattn_Wk',
        'L0_xattn_bk', 'L0_xattn_Wv', 'L0_xattn_bv', 'L0_ffn_w_router', 'L0_ffn_W1', 'L0_ffn_b1', 'L0_ffn_W2',
        'L0_ffn_b2']
_OUTS = [((8, 1024, 512), 'float32')]


def kernel(**inputs):
    import numpy as _np
    import concourse.bacc as _bacc
    from concourse import mybir as _mybir
    from concourse.bass_utils import run_bass_kernel_spmd as _run

    nc = _bacc.Bacc("TRN2", target_bir_lowering=False, num_devices=1)
    arrays, args = {}, []
    for name in _INS:
        a = _np.ascontiguousarray(inputs[name])
        arrays[f"in_{name}_dram"] = a
        args.append(nc.dram_tensor(f"in_{name}_dram", a.shape, _mybir.dt.from_np(a.dtype), kind="ExternalInput").ap())
    for i, (shape, dtype) in enumerate(_OUTS):
        dt = _mybir.dt.from_np(_np.dtype(dtype))
        args.append(nc.dram_tensor(f"out_{i}_dram", shape, dt, kind="ExternalOutput").ap())
    flamingo_gated_layer(nc, *args)
    r = _run(nc, [arrays], core_ids=[0])
    return r.results[0]["out_0_dram"]
```

```python
from contextlib import ExitStack

import concourse.bass as bass
from concourse import mybir

F32 = mybir.dt.float32
F16 = mybir.dt.float16
U8 = mybir.dt.uint8
I32 = mybir.dt.int32
U32 = mybir.dt.uint32
ALU = mybir.AluOpType
ACT = mybir.ActivationFunctionType
AX = mybir.AxisListType

P = 128
BANK = 512
EPS = 1e-5

S_LN = 2.0 ** 2
S_A = 2.0 ** 4
S_W = 2.0 ** 8
S_Q = S_LN * S_A
S_CTX = 2.0 ** 4
S_P = 2.0 ** 12
S_OUT = 2.0 ** -2
S_G = 2.0 ** 6

MASKED = -3.0e38
FLOOR = -1.0e30
FAR = 1.0e6


class Bank:

    def __init__(self, index, n, per, split_n, split_per):
        self.index, self.n, self.per, self.split_n, self.split_per = index, n, per, split_n, split_per

    def use(self, batch):
        return batch * self.per + self.n

    def split(self, batch):
        return batch * self.split_per + self.split_n


def share_banks(steps, banks, is_split):
    uses = {b: 0 for b in banks}
    splits = {b: 0 for b in banks}
    dealt = []
    for k, step in enumerate(steps):
        b = banks[k % len(banks)]
        uses[b] += 1
        splits[b] += is_split(step)
        dealt.append((step, b, uses[b], splits[b]))
    return {step: Bank(b, n, uses[b], m, splits[b]) for step, b, n, m in dealt}


def wait_apart(eng, sem, value, passed):
    eng.wait_ge(sem, value)
    eng.sem_inc(passed, 1)


def flamingo_gated_layer(nc, x, ctx_in, mask, g_xattn, g_ffn, Wq, bq, Wk, bk, Wv, bv, w_router, W1, b1, W2, b2, out):
    B, S, D = x.shape
    K = ctx_in.shape[1]
    F = W1.shape[1]
    TOP = S // 2
    DC = D // P
    QT = S // P
    HALF = S // 2
    KB = (K + P - 1) // P
    TAIL = KB - 1
    TW = K - TAIL * P
    CB = 3
    NCH = TAIL // CB
    LEAD = NCH - 1
    CW = CB * P
    FT = F // P
    ST = TOP // P
    assert TAIL % CB == 0 and D == BANK and TOP == BANK and CW <= BANK
    K_EXP = 1.0 / (D ** 0.5) / (S_Q * S_CTX)

    h2_rows = nc.dram_tensor("h2_rows", [B * S, D], F32, kind="Internal").ap()
    slot_table = nc.dram_tensor("slot_table", [B * TOP, 2], F32, kind="Internal").ap()
    out_rows = out.rearrange("b s d -> (b s) d")

    with ExitStack() as whole:
        def keep(name, shape, dt):
            return whole.enter_context(nc.sbuf_tensor(name, shape, dt))

        def sem(name):
            return whole.enter_context(nc.semaphore(name))

        ps = [whole.enter_context(nc.psum_tensor(f"bank{k}", [P, BANK], F32)) for k in range(8)]
        ident = keep("ident", [P, P], F32)
        unseen = keep("unseen", [P, QT, K], U8)
        a_hi = keep("a_hi", [P, DC, D], F16)
        a_lo = keep("a_lo", [P, DC, D], F16)
        wv_hi = keep("wv_hi", [P, DC, D], F16)
        wv_lo = keep("wv_lo", [P, DC, D], F16)
        q_bias = keep("q_bias", [P, DC], F32)
        r_hi = keep("r_hi", [P, DC], F16)
        r_lo = keep("r_lo", [P, DC], F16)
        r_bias = keep("r_bias", [P, 1], F32)
        tanh_x = keep("tanh_x", [P, 1], F32)
        tanh_f = keep("tanh_f", [P, 1], F32)
        bv_row = keep("bv_row", [P, D], F32)
        router_row = keep("router_row", [P, D], F32)
        minus_half = keep("minus_half", [P, 1], F32)
        seen_flags = keep("seen_flags", [1, NCH + 1], I32)
        router = keep("router", [P, B * QT], F32)

        waits_passed = sem("waits_passed")

        with ExitStack() as part:
            def sb(name, shape, dt):
                return part.enter_context(nc.sbuf_tensor(name, shape, dt))

            wq_in = sb("wq_in", [P, DC, D], F32)
            wk_in = sb("wk_in", [P, DC, D], F32)
            wv_in = sb("wv_in", [P, DC, D], F32)
            wqT = sb("wqT", [P, DC, D], F32)
            wkT = sb("wkT", [P, DC, D], F32)
            mask_in = sb("mask_in", [P, QT, K], U8)
            bq_col = sb("bq_col", [P, DC], F32)
            bk_col = sb("bk_col", [P, DC], F32)
            gx_col = sb("gx_col", [P, 1], F32)
            gf_col = sb("gf_col", [P, 1], F32)
            tanh_gx = sb("tanh_gx", [P, 1], F32)
            bv_in = sb("bv_in", [P, D], F32)
            seen_part = sb("seen_part", [P, NCH], F32)
            seen_any = sb("seen_any", [P, NCH], F32)
            ones = sb("ones", [P, P], F32)

            s_wqk = sem("setup_wqk_loaded")
            s_small = sem("setup_small_loaded")
            s_wv = sem("setup_wv_loaded")
            s_mask = sem("setup_mask_loaded")
            s_ones = sem("setup_ones")
            s_ident = sem("setup_ident")
            s_turned = sem("setup_turned")
            s_copied = sem("setup_copied")
            s_mm = sem("setup_products")
            s_hi = sem("setup_hi")
            s_lo = sem("setup_lo")
            s_tanh = sem("setup_tanh")
            s_part = sem("setup_seen_part")
            s_any = sem("setup_seen_any")
            s_const = sem("setup_const")

            with nc.Block() as block:
                @block.sync
                def _(sp):
                    sp.dma_start(wq_in[:], Wq.rearrange("(c p) e -> p c e", p=P)).then_inc(s_wqk, 16)
                    sp.dma_start(wk_in[:], Wk.rearrange("(c p) e -> p c e", p=P)).then_inc(s_wqk, 16)
                    sp.dma_start(mask_in[:], mask.rearrange("(t p) k -> p t k", p=P)).then_inc(s_mask, 16)
                    sp.dma_start(wv_in[:], Wv.rearrange("(c p) e -> p c e", p=P)).then_inc(s_wv, 16)

                @block.gpsimd
                def _(pool):
                    nc.gpsimd.memset(ones[:], 1.0).then_inc(s_ones, 1)
                    pool.wait_ge(s_ones, 1)
                    nc.gpsimd.affine_select(out=ident[:], in_=ones[:], compare_op=ALU.is_equal, fill=0.0,
                                            base=0, pattern=[[-1, P]], channel_multiplier=1).then_inc(s_ident, 1)
                    nc.gpsimd.memset(minus_half[:], -0.5).then_inc(s_const, 1)
                    pool.wait_ge(s_part, NCH)
                    nc.gpsimd.partition_all_reduce(seen_any[:], seen_part[:], P,
                                                   bass.bass_isa.ReduceOp.max).then_inc(s_any, 1)

                @block.scalar
                def _(act):
                    with nc.allow_non_contiguous_dma(reason="a few hundred bias values, once"):
                        act.dma_start(bq_col[:], bq.rearrange("(c p) -> p c", p=P)).then_inc(s_small, 16)
                        act.dma_start(bk_col[:], bk.rearrange("(c p) -> p c", p=P)).then_inc(s_small, 16)
                    act.dma_start(gx_col[:], g_xattn.partition_broadcast(P)).then_inc(s_small, 16)
                    act.dma_start(gf_col[:], g_ffn.partition_broadcast(P)).then_inc(s_small, 16)
                    act.dma_start(bv_in[:], bv.partition_broadcast(P)).then_inc(s_small, 16)
                    act.dma_start(router_row[:], w_router.partition_broadcast(P)).then_inc(s_small, 16)
                    act.wait_ge(s_small, 96)
                    nc.scalar.activation(tanh_gx[:], gx_col[:], ACT.Tanh).then_inc(s_tanh, 1)
                    nc.scalar.activation(tanh_f[:], gf_col[:], ACT.Tanh).then_inc(s_tanh, 1)
                    act.wait_ge(s_wv, 16)
                    nc.scalar.activation(wv_hi[:], wv_in[:], ACT.Copy, scale=S_W).then_inc(s_hi, 1)
                    for c in range(DC):
                        act.wait_ge(s_mm, c + 1)
                        nc.scalar.activation(a_hi[:, c, :], ps[c][:], ACT.Copy, scale=S_A).then_inc(s_hi, 1)
                    act.wait_ge(s_mm, DC + 2)
                    nc.scalar.activation(r_hi[:], ps[5][:, 0:DC], ACT.Copy, scale=S_W).then_inc(s_hi, 1)
                    act.wait_ge(s_mask, 16)
                    nc.scalar.activation(unseen[:], mask_in[:], ACT.Copy, scale=-1.0, bias=1.0).then_inc(s_hi, 1)

                @block.tensor
                def _(pe):
                    pe.wait_ge(s_ident, 1)
                    pe.wait_ge(s_wqk, 32)
                    for n, w in enumerate((wq_in, wk_in)):
                        for f in range(DC):
                            for d in range(DC):
                                last = pe.transpose(ps[4 * n + f][:, d * P:(d + 1) * P],
                                                    w[:, d, f * P:(f + 1) * P], ident[:])
                            last.then_inc(s_turned, 1)
                    pe.wait_ge(s_copied, 2 * DC)
                    for d in range(DC):
                        for f in range(DC):
                            last = pe.matmul(ps[d][:], wqT[:, f, d * P:(d + 1) * P], wkT[:, f, :],
                                             start=(f == 0), stop=(f == DC - 1))
                        last.then_inc(s_mm, 1)
                    pe.wait_ge(s_small, 96)
                    for bank, w, col in ((4, wkT, bq_col), (5, wqT, bk_col)):
                        for d in range(DC):
                            for f in range(DC):
                                last = pe.matmul(ps[bank][:, d:d + 1], w[:, f, d * P:(d + 1) * P],
                                                 col[:, f:f + 1], start=(f == 0), stop=(f == DC - 1))
                        last.then_inc(s_mm, 1)
                    for f in range(DC):
                        last = pe.matmul(ps[6][:, 0:1], bq_col[:, f:f + 1].to_broadcast([P, P]),
                                         bk_col[:, f:f + 1], start=(f == 0), stop=(f == DC - 1))
                    last.then_inc(s_mm, 1)

                @block.vector
                def _(dve):
                    for n, w in enumerate((wqT, wkT)):
                        for f in range(DC):
                            dve.wait_ge(s_turned, DC * n + f + 1)
                            nc.vector.tensor_copy(w[:, f, :], ps[4 * n + f][:]).then_inc(s_copied, 1)
                    dve.wait_ge(s_mask, 16)
                    for c in range(NCH):
                        nc.vector.tensor_reduce(seen_part[:, c:c + 1], mask_in[:, :, c * CW:(c + 1) * CW],
                                                AX.XY, ALU.max).then_inc(s_part, 1)
                    dve.wait_ge(s_hi, 1)
                    nc.vector.scalar_tensor_tensor(out=wv_lo[:], in0=wv_in[:], scalar=S_W, in1=wv_hi[:],
                                                   op0=ALU.mult, op1=ALU.subtract).then_inc(s_lo, 1)
                    for c in range(DC):
                        dve.wait_ge(s_hi, c + 2)
                        nc.vector.scalar_tensor_tensor(out=a_lo[:, c, :], in0=ps[c][:], scalar=S_A,
                                                       in1=a_hi[:, c, :], op0=ALU.mult,
                                                       op1=ALU.subtract).then_inc(s_lo, 1)
                    dve.wait_ge(s_mm, DC + 1)
                    nc.vector.tensor_scalar(q_bias[:], ps[4][:, 0:DC], S_Q, None, ALU.mult).then_inc(s_lo, 1)
                    dve.wait_ge(s_hi, DC + 2)
                    nc.vector.scalar_tensor_tensor(out=r_lo[:], in0=ps[5][:, 0:DC], scalar=S_W, in1=r_hi[:],
                                                   op0=ALU.mult, op1=ALU.subtract).then_inc(s_lo, 1)
                    dve.wait_ge(s_mm, DC + 3)
                    nc.vector.tensor_scalar(r_bias[:], ps[6][:, 0:1], S_Q * S_CTX, None,
                                            ALU.mult).then_inc(s_lo, 1)
                    dve.wait_ge(s_tanh, 2)
                    nc.vector.tensor_scalar(tanh_x[:], tanh_gx[:], 1.0 / (S_OUT * S_W), None,
                                            ALU.mult).then_inc(s_lo, 1)
                    nc.vector.tensor_scalar(bv_row[:], bv_in[:], tanh_gx[:], None, ALU.mult).then_inc(s_lo, 1)
                    dve.wait_ge(s_any, 1)
                    nc.vector.tensor_copy(seen_flags[:, 0:NCH], seen_any[0:1, :]).then_inc(s_lo, 1)
                    nc.vector.tensor_reduce(seen_flags[:, NCH:NCH + 1], seen_any[0:1, 0:LEAD], AX.X,
                                            ALU.max).then_inc(s_lo, 1)

        with ExitStack() as part:
            def sb(name, shape, dt):
                return part.enter_context(nc.sbuf_tensor(name, shape, dt))

            def psem(name):
                return part.enter_context(nc.semaphore(name))

            x_in = [sb(f"x_in{s}", [P, D], F32) for s in range(2)]
            x_res = [sb(f"x_res{s}", [P, D], F32) for s in range(4)]
            h2 = [sb(f"h2_{s}", [P, D], F32) for s in range(2)]
            hT_hi = sb("hT_hi", [P, DC, S], F16)
            hT_lo = sb("hT_lo", [P, DC, S], F16)
            qT_hi = sb("qT_hi", [P, DC, S], F16)
            qT_lo = sb("qT_lo", [P, DC, S], F16)
            prob = [sb(f"prob{s}", [P, K], F32) for s in range(2)]
            pT_hi = sb("pT_hi", [P, KB, S], F16)
            pT_lo = sb("pT_lo", [P, KB, S], F16)
            c_in = [sb(f"c_in{s}", [P, D], F32) for s in range(4)]
            c_hi = sb("c_hi", [P, KB, D], F16)
            c_lo = sb("c_lo", [P, KB, D], F16)
            cT_hi = sb("cT_hi", [P, DC, K + 1], F16)
            cT_lo = sb("cT_lo", [P, DC, K + 1], F16)
            st1 = [sb(f"st1_{s}", [P, 6], F32) for s in range(2)]
            mv1 = [sb(f"mv1_{s}", [P, 2], F32) for s in range(2)]
            rs1 = [sb(f"rs1_{s}", [P, 1], F32) for s in range(2)]
            st2 = [sb(f"st2_{s}", [P, 6], F32) for s in range(4)]
            mv2 = [sb(f"mv2_{s}", [P, 2], F32) for s in range(4)]
            rs2 = [sb(f"rs2_{s}", [P, 1], F32) for s in range(4)]
            shift2 = [sb(f"shift2_{s}", [P, 1], F32) for s in range(4)]
            y_mul = [sb(f"y_mul{s}", [P, 1], F32) for s in range(4)]
            y_add = [sb(f"y_add{s}", [P, 1], F32) for s in range(4)]
            r_all = sb("r_all", [P, QT], F32)
            cmax = [sb(f"cmax{s}", [P, NCH + 1], F32) for s in range(2)]
            csum = [sb(f"csum{s}", [P, NCH + 1], F32) for s in range(2)]
            rmax = [sb(f"rmax_{s}", [P, 1], F32) for s in range(2)]
            smax = [sb(f"smax_{s}", [P, 1], F32) for s in range(2)]
            shift = [sb(f"shift{s}", [P, 1], F32) for s in range(2)]
            rsum = [sb(f"rsum_{s}", [P, 1], F32) for s in range(2)]
            rinv = [sb(f"rinv_{s}", [P, 1], F32) for s in range(2)]
            o_scale = sb("o_scale", [P, QT], F32)
            junk = sb("junk", [P, D], F16)
            router8 = sb("router8", [P, QT], F32)

            full = [psem(f"bank_full{k}") for k in range(8)]
            hi_out = [psem(f"bank_hi_out{k}") for k in range(8)]
            drained = [psem(f"bank_drained{k}") for k in range(8)]
            x_loaded = [psem(f"x_loaded{s}") for s in range(2)]
            xres_loaded = [psem(f"xres_loaded{s}") for s in range(4)]
            y_stored = [psem(f"y_stored{s}") for s in range(4)]
            h2_stored = [psem(f"h2_stored{s}") for s in range(2)]
            c_loaded = [psem(f"c_loaded{s}") for s in range(4)]
            c_used = [psem(f"c_used{s}") for s in range(4)]
            ln1_stats = psem("ln1_stats")
            ln1_moments = psem("ln1_moments")
            ln1_eps = psem("ln1_eps")
            ln1_rstd = psem("ln1_rstd")
            h_ready = psem("h_ready")
            chunk_max = psem("chunk_max")
            row_max = psem("row_max")
            held_max = psem("held_max")
            shift_ready = psem("shift_ready")
            probs_ready = psem("probs_ready")
            row_sum = psem("row_sum")
            row_inv = psem("row_inv")
            scale_ready = psem("scale_ready")
            xbias_ready = psem("xbias_ready")
            ln2_stats = psem("ln2_stats")
            ln2_moments = psem("ln2_moments")
            ln2_eps = psem("ln2_eps")
            ln2_rstd = psem("ln2_rstd")
            ln2_shift = psem("ln2_shift")
            y_affine = psem("y_affine")
            h2_ready = psem("h2_ready")
            y_ready = psem("y_ready")
            r_done = psem("router_tile_done")
            r_kept = psem("router_kept")
            presets = psem("presets")

            def early_first():
                steps = [("stats", 0), ("stats", 1)]
                for t in range(QT):
                    steps += [("norm", t), ("hT", t)]
                    if t + 2 < QT:
                        steps.append(("stats", t + 2))
                return steps

            def main_steps(prepare):
                e = prepare

                def contexts(h):
                    t = 4 * h
                    return ([("OT", h, 0)] + e * [("norm", t)] + [("OT", h, 1)]
                            + e * [("hT", t), ("norm", t + 1)] + [("OT", h, 2)]
                            + e * [("stats", t + 2), ("hT", t + 1)] + [("OT", h, 3)]
                            + e * [("norm", t + 2), ("stats", t + 3), ("hT", t + 2)])

                steps, left = [], KB
                for k in range(2 * DC):
                    steps.append(("Q", k // DC, k % DC))
                    n = -(-left // (2 * DC - k))
                    steps += [("ctx", j) for j in range(KB - left, KB - left + n)]
                    left -= n
                steps.append(("R",))
                for t in range(QT):
                    steps.append(("S", t))
                    if t > 0:
                        steps.append(("PT", t - 1))
                steps += e * [("stats", 0), ("stats", 1)]
                steps += contexts(0) + [("PT", QT - 1)] + e * [("norm", 3)] + [("O", 0)] + e * [("hT", 3)]
                for t in range(1, 4):
                    steps += [("O", t), ("Y", t - 1)] + e * (t > 1) * [("stats", t + 2)]
                steps += contexts(1)
                steps += e * [("norm", 7)] + [("Y", 3)] + e * [("hT", 7)]
                for t in range(4, QT):
                    steps.append(("O", t))
                    if t > 4:
                        steps.append(("Y", t - 1))
                return steps + [("Y", QT - 1)]

            def groups_main():
                out_ = []
                for s in main_steps(False):
                    if s[0] in ("S", "PT"):
                        out_ += [s + (c,) for c in range(NCH + 1)]
                    elif s[0] in ("Q", "R", "OT", "O"):
                        out_.append(s)
                return out_

            at = share_banks(groups_main(), [0, 1, 2, 3, 4, 5], lambda s: s[0] in ("Q", "PT", "OT"))
            at.update(share_banks([s for s in early_first() if s[0] == "hT"] + [("ctx", j) for j in range(KB)], [6, 7],
                                  lambda s: True))
            c_uses = [len(range(s, KB, 4)) for s in range(4)]

            def turn(b, t):
                return b * QT + t + 1

            def is_drained(eng, step, b):
                g = at[step]
                eng.wait_ge(drained[g.index], g.use(b) + 1)

            def is_full(eng, step, b):
                g = at[step]
                eng.wait_ge(full[g.index], g.use(b))

            def is_free(eng, step, b):
                g = at[step]
                eng.wait_ge(drained[g.index], g.use(b))

            def hi_is_out(eng, step, b):
                g = at[step]
                eng.wait_ge(hi_out[g.index], g.split(b))

            def over_chunks(eng, seen, taken, passed=None):
                def one(c):
                    with eng.If(seen[c] > 0):
                        taken(c)
                    if passed:
                        with eng.Else():
                            passed(c)
                with eng.If(seen[NCH] > 0):
                    for c in range(LEAD):
                        one(c)
                if passed:
                    with eng.Else():
                        for c in range(LEAD):
                            passed(c)
                for c in range(LEAD, NCH):
                    one(c)

            def blocks_of(c):
                return range(c * CB, (c + 1) * CB) if c < NCH else range(TAIL, KB)

            def cols(c):
                return slice(c * CW, (c + 1) * CW) if c < NCH else slice(TAIL * P, K)

            def over_batches(eng, early, main):
                early(0)
                with eng.Fori(0, B - 1) as b:
                    main(b, main_steps(True))
                main(B - 1, main_steps(False))

            with nc.Block() as block:
                @block.sync
                def _(sp):
                    def load_x(b, t):
                        sp.dma_start(x_in[t % 2][:], x[bass.ds(b, 1), t * P:(t + 1) * P, :]
                                     .rearrange("o p d -> p (o d)")).then_inc(x_loaded[t % 2], 16)

                    seen = [sp.value_load(seen_flags[0:1, c:c + 1], min_val=0, max_val=1) for c in range(NCH)]

                    def load_c(b, j, used):
                        rows = P if j < TAIL else TW

                        def slot_free():
                            if not isinstance(used, int) or used > 0:
                                sp.wait_ge(c_used[j % 4], used)

                        def load():
                            slot_free()
                            sp.dma_start(c_in[j % 4][0:rows, :], ctx_in[bass.ds(b, 1), j * P:j * P + rows, :]
                                         .rearrange("o p d -> p (o d)")).then_inc(c_loaded[j % 4], 16)
                        if j == TAIL:
                            load()
                        else:
                            with sp.If(seen[j // CB] > 0):
                                load()
                            with sp.Else():
                                slot_free()
                                sp.sem_inc(c_loaded[j % 4], 16)

                    def load_xres(b, t):
                        sp.wait_ge(y_stored[t % 4], 16 * (QT // 4 * b + t // 4 + 1))
                        sp.dma_start(x_res[t % 4][:], x[bass.ds(b, 1), t * P:(t + 1) * P, :]
                                     .rearrange("o p d -> p (o d)")).then_inc(xres_loaded[t % 4], 16)

                    def early_step(b, s):
                        if s[0] == "hT" and s[1] + 2 < QT:
                            is_drained(sp, s, b)
                            load_x(b, s[1] + 2)

                    def early(b):
                        for t in range(2):
                            load_x(b, t)
                        for j in range(4):
                            load_c(b, j, 0)
                        for s in early_first():
                            early_step(b, s)

                    def main(b, steps):
                        prepare = ("hT", 0) in steps
                        for j in range(4, KB):
                            load_c(b, j, c_uses[j % 4] * b + j // 4)
                        if prepare:
                            is_full(sp, ("Q", 0, 0), b)
                            for t in range(2):
                                load_x(b + 1, t)
                            for j in range(4):
                                load_c(b + 1, j, c_uses[j] * (b + 1))
                        for t in range(4):
                            load_xres(b, t)
                        for s in steps:
                            if s[0] == "hT":
                                early_step(b + 1, s)
                            if s[0] == "Y":
                                t = s[1]
                                sp.wait_ge(h2_ready, turn(b, t))
                                sp.dma_start(h2_rows[bass.ds(b * S + t * P, P), :],
                                             h2[t % 2][:]).then_inc(h2_stored[t % 2], 16)
                                sp.wait_ge(y_ready, turn(b, t))
                                sp.dma_start(out_rows[bass.ds(b * S + t * P, P), :],
                                             x_res[t % 4][:]).then_inc(y_stored[t % 4], 16)
                                if t + 4 < QT:
                                    load_xres(b, t + 4)

                    over_batches(sp, early, main)
                    for s in range(4):
                        sp.wait_ge(y_stored[s], 16 * (QT // 4 * B + 1))
                    for s in range(2):
                        sp.wait_ge(h2_stored[s], 16 * (QT // 2 * B + 1))

                @block.gpsimd
                def _(pool):
                    for s in range(2):
                        nc.gpsimd.memset(cmax[s][:], MASKED).then_inc(presets, 1)
                        nc.gpsimd.memset(csum[s][:], 0.0).then_inc(presets, 1)
                    for s in range(4):
                        pool.sem_inc(y_stored[s], 16)
                    for s in range(2):
                        pool.sem_inc(h2_stored[s], 16)

                    def rstd(b, t, mv, rs, moments, eps_in, ready):
                        wait_apart(pool, moments, turn(b, t), waits_passed)
                        nc.gpsimd.tensor_scalar(rs[:], mv[:, 1:2], EPS, None, ALU.add).then_inc(eps_in, 1)
                        pool.wait_ge(eps_in, turn(b, t))
                        nc.gpsimd.tensor_tensor(rs[:], rs[:], minus_half[:], ALU.pow).then_inc(ready, 1)

                    def step(b, s):
                        if s[0] == "stats":
                            t = s[1]
                            rstd(b, t, mv1[t % 2], rs1[t % 2], ln1_moments, ln1_eps, ln1_rstd)

                    def early(b):
                        for s in early_first():
                            step(b, s)

                    def main(b, steps):
                        for s in steps:
                            if s[0] == "O":
                                t = s[1]
                                pool.wait_ge(xres_loaded[t % 4], 16 * (QT // 4 * b + t // 4 + 1))
                                nc.gpsimd.tensor_tensor(x_res[t % 4][:], x_res[t % 4][:], bv_row[:],
                                                        ALU.add).then_inc(xbias_ready, 1)
                                rstd(b, t, mv2[t % 4], rs2[t % 4], ln2_moments, ln2_eps, ln2_rstd)
                                wait_apart(pool, ln2_rstd, turn(b, t), waits_passed)
                                nc.gpsimd.tensor_scalar(shift2[t % 4][:], mv2[t % 4][:, 0:1], rs2[t % 4][:], -1.0,
                                                        ALU.mult, ALU.mult).then_inc(ln2_shift, 1)
                                nc.gpsimd.tensor_scalar(y_mul[t % 4][:], rs2[t % 4][:], tanh_f[:], 1.0, ALU.mult,
                                                        ALU.add)
                                wait_apart(pool, ln2_shift, turn(b, t), waits_passed)
                                nc.gpsimd.tensor_scalar(y_add[t % 4][:], shift2[t % 4][:], tanh_f[:], None,
                                                        ALU.mult).then_inc(y_affine, 1)
                            else:
                                step(b + 1, s)

                    over_batches(pool, early, main)

                @block.tensor
                def _(pe):
                    seen = [pe.value_load(seen_flags[0:1, c:c + 1], min_val=0, max_val=1) for c in range(NCH + 1)]

                    def products(dst, pairs, start=True, stop=True):
                        n = 3 * len(pairs)
                        k = 0
                        for sh, sl, mh, ml in pairs:
                            for st, mo in ((sh, mh), (sh, ml), (sl, mh)):
                                last = pe.matmul(dst, st, mo, start=start and k == 0,
                                                 stop=stop and k == n - 1, skip_group_check=True)
                                k += 1
                        return last

                    def Q(b, s):
                        _, h, c = s
                        g = at[s]
                        is_drained(pe, ("hT", 4 * h + 3), b)
                        is_free(pe, s, b)
                        e = slice(c * P, (c + 1) * P)
                        q = slice(h * HALF, (h + 1) * HALF)
                        products(ps[g.index][:], [(a_hi[:, d, e], a_lo[:, d, e], hT_hi[:, d, q], hT_lo[:, d, q])
                                                  for d in range(DC)]).then_inc(full[g.index], 1)

                    def R(b, s):
                        g = at[s]
                        is_free(pe, s, b)
                        for t in range(QT):
                            q = slice(t * P, (t + 1) * P)
                            last = products(ps[g.index][:, t:t + 1],
                                            [(hT_hi[:, d, q], hT_lo[:, d, q], r_hi[:, d:d + 1], r_lo[:, d:d + 1])
                                             for d in range(DC)])
                        last.then_inc(full[g.index], 1)

                    def scores(b, s, c):
                        t = s[1]
                        g = at[s + (c,)]
                        q = slice(t * P, (t + 1) * P)
                        return products(ps[g.index][:, 0:(CW if c < NCH else TW)],
                                        [(qT_hi[:, d, q], qT_lo[:, d, q], cT_hi[:, d, cols(c)], cT_lo[:, d, cols(c)])
                                         for d in range(DC)])

                    def pass_on(b, s, c):
                        is_free(pe, s + (c,), b)
                        pe.sem_inc(full[at[s + (c,)].index], 1)

                    def S_(b, s):
                        t = s[1]
                        if t == 0:
                            pe.wait_ge(c_used[TAIL % 4], c_uses[TAIL % 4] * (b + 1))
                        if t % 4 == 0:
                            is_drained(pe, ("Q", t // 4, DC - 1), b)

                        def taken(c):
                            is_free(pe, s + (c,), b)
                            scores(b, s, c).then_inc(full[at[s + (c,)].index], 1)

                        over_chunks(pe, seen, taken, lambda c: pass_on(b, s, c))
                        g = at[s + (NCH,)]
                        is_free(pe, s + (NCH,), b)
                        scores(b, s, NCH).then_inc(full[g.index], 1)

                    def turned(s, c):
                        t = s[1]
                        g = at[s + (c,)]
                        for k, j in enumerate(blocks_of(c)):
                            w = P if j < TAIL else TW
                            last = pe.transpose(ps[g.index][0:w, k * P:(k + 1) * P],
                                                prob[t % 2][:, j * P:j * P + w], ident[:])
                        return last

                    def PT(b, s):
                        pe.wait_ge(probs_ready, turn(b, s[1]))

                        def taken(c):
                            is_free(pe, s + (c,), b)
                            turned(s, c).then_inc(full[at[s + (c,)].index], 1)

                        over_chunks(pe, seen, taken, lambda c: pass_on(b, s, c))
                        g = at[s + (NCH,)]
                        is_free(pe, s + (NCH,), b)
                        turned(s, NCH).then_inc(full[g.index], 1)

                    def OT(b, s):
                        _, h, c = s
                        g = at[s]
                        if c == 0:
                            is_drained(pe, ("PT", 4 * h + 3, NCH), b)
                        is_free(pe, s, b)
                        e = slice(c * P, (c + 1) * P)
                        q = slice(h * HALF, (h + 1) * HALF)
                        dst = ps[g.index][:]

                        def pair(j, w):
                            return c_hi[0:w, j, e], c_lo[0:w, j, e], pT_hi[0:w, j, q], pT_lo[0:w, j, q]

                        th, tl, ph, pl = pair(TAIL, TW)
                        pe.matmul(dst, th, ph, start=True, stop=False, skip_group_check=True)
                        over_chunks(pe, seen, lambda k: products(dst, [pair(j, P) for j in blocks_of(k)],
                                                                 start=False, stop=False))
                        pe.matmul(dst, th, pl, start=False, stop=False, skip_group_check=True)
                        pe.matmul(dst, tl, ph, start=False, stop=True,
                                  skip_group_check=True).then_inc(full[g.index], 1)

                    def O(b, s):
                        t = s[1]
                        g = at[s]
                        if t % 4 == 0:
                            is_drained(pe, ("OT", t // 4, DC - 1), b)
                        is_free(pe, s, b)
                        q = slice(t * P, (t + 1) * P)
                        products(ps[g.index][:], [(qT_hi[:, d, q], qT_lo[:, d, q], wv_hi[:, d, :], wv_lo[:, d, :])
                                                  for d in range(DC)]).then_inc(full[g.index], 1)

                    def hT(b, s):
                        t = s[1]
                        g = at[s]
                        pe.wait_ge(h_ready, turn(b, t))
                        is_free(pe, s, b)
                        for d in range(DC):
                            last = pe.transpose(ps[g.index][:, d * P:(d + 1) * P],
                                                x_in[t % 2][:, d * P:(d + 1) * P], ident[:])
                        last.then_inc(full[g.index], 1)

                    def ctx_turned(s):
                        j = s[1]
                        g = at[s]
                        w = P if j < TAIL else TW
                        for d in range(DC):
                            last = pe.transpose(ps[g.index][:, d * P:d * P + w],
                                                c_in[j % 4][0:w, d * P:(d + 1) * P], ident[0:w, 0:w])
                        return last

                    def ctx(b, s):
                        j = s[1]
                        g = at[s]
                        pe.wait_ge(c_loaded[j % 4], 16 * (c_uses[j % 4] * b + j // 4 + 1))
                        is_free(pe, s, b)
                        if j == TAIL:
                            ctx_turned(s).then_inc(full[g.index], 1)
                        else:
                            with pe.If(seen[j // CB] > 0):
                                ctx_turned(s).then_inc(full[g.index], 1)
                            with pe.Else():
                                pe.sem_inc(full[g.index], 1)

                    does = {"Q": Q, "R": R, "S": S_, "PT": PT, "OT": OT, "O": O, "ctx": ctx}
                    does_early = {"hT": hT}

                    def early(b):
                        for s in early_first():
                            if s[0] in does_early:
                                does_early[s[0]](b, s)

                    def main(b, steps):
                        for s in steps:
                            if s[0] in does:
                                does[s[0]](b, s)
                            elif s[0] in does_early:
                                does_early[s[0]](b + 1, s)

                    over_batches(pe, early, main)

                @block.scalar
                def _(act):
                    seen = [act.value_load(seen_flags[0:1, c:c + 1], min_val=0, max_val=1) for c in range(NCH + 1)]
                    act.wait_ge(presets, 4)

                    def Q(b, s):
                        _, h, c = s
                        g = at[s]
                        is_full(act, s, b)
                        nc.scalar.activation(qT_hi[:, c, h * HALF:(h + 1) * HALF], ps[g.index][:], ACT.Identity,
                                             bias=q_bias[:, c:c + 1]).then_inc(hi_out[g.index], 1)

                    def S_(b, s):
                        t = s[1]

                        def exp(c):
                            act.wait_ge(shift_ready, turn(b, t))
                            return nc.scalar.activation(prob[t % 2][:, cols(c)], prob[t % 2][:, cols(c)], ACT.Exp,
                                                        bias=shift[t % 2][:], scale=K_EXP,
                                                        accum_out=csum[t % 2][:, c:c + 1])
                        over_chunks(act, seen, exp)
                        exp(NCH).then_inc(probs_ready, 1)

                    def PT(b, s):
                        t = s[1]
                        q = slice(t * P, (t + 1) * P)

                        def taken(c):
                            g = at[s + (c,)]
                            is_full(act, s + (c,), b)
                            nc.scalar.activation(pT_hi[:, c * CB:(c + 1) * CB, q],
                                                 ps[g.index][:, 0:CW].rearrange("p (j q) -> p j q", j=CB),
                                                 ACT.Copy, scale=S_P).then_inc(hi_out[g.index], 1)

                        def passed(c):
                            is_full(act, s + (c,), b)
                            act.sem_inc(hi_out[at[s + (c,)].index], 1)

                        over_chunks(act, seen, taken, passed)
                        g = at[s + (NCH,)]
                        is_full(act, s + (NCH,), b)
                        nc.scalar.activation(pT_hi[0:TW, TAIL, q], ps[g.index][0:TW, 0:P],
                                             ACT.Copy, scale=S_P).then_inc(hi_out[g.index], 1)

                    def OT(b, s):
                        _, h, c = s
                        g = at[s]
                        is_full(act, s, b)
                        nc.scalar.activation(qT_hi[:, c, h * HALF:(h + 1) * HALF], ps[g.index][:], ACT.Copy,
                                             scale=S_OUT / (S_P * S_CTX)).then_inc(hi_out[g.index], 1)

                    def Y(b, s):
                        t = s[1]
                        xr = x_res[t % 4]
                        act.wait_ge(y_affine, turn(b, t))
                        act.wait_ge(h2_stored[t % 2], 16 * (QT // 2 * b + t // 2 + 1))
                        act.wait_ge(r_done, turn(b, t))
                        nc.scalar.activation(h2[t % 2][:], xr[:], ACT.Identity, bias=shift2[t % 4][:],
                                             scale=rs2[t % 4][:]).then_inc(h2_ready, 1)
                        act.wait_ge(h2_ready, turn(b, t))
                        nc.scalar.activation(xr[:], xr[:], ACT.Identity, bias=y_add[t % 4][:],
                                             scale=y_mul[t % 4][:]).then_inc(y_ready, 1)

                    def hT(b, s):
                        t = s[1]
                        g = at[s]
                        is_full(act, s, b)
                        nc.scalar.activation(hT_hi[:, :, t * P:(t + 1) * P],
                                             ps[g.index][:].rearrange("p (c q) -> p c q", c=DC),
                                             ACT.Copy, scale=S_LN).then_inc(hi_out[g.index], 1)

                    def ctx(b, s):
                        j = s[1]
                        g = at[s]
                        w = P if j < TAIL else TW

                        def arrived():
                            act.wait_ge(c_loaded[j % 4], 16 * (c_uses[j % 4] * b + j // 4 + 1))
                            is_full(act, s, b)

                        def split():
                            arrived()
                            nc.scalar.activation(cT_hi[:, :, j * P:j * P + w],
                                                 ps[g.index][:].rearrange("p (c k) -> p c k", c=DC)[:, :, 0:w],
                                                 ACT.Copy, scale=S_CTX)
                            nc.scalar.activation(c_hi[0:w, j, :], c_in[j % 4][0:w, :], ACT.Copy,
                                                 scale=S_CTX).then_inc(hi_out[g.index], 1)
                        if j == TAIL:
                            split()
                        else:
                            with act.If(seen[j // CB] > 0):
                                split()
                            with act.Else():
                                arrived()
                                act.sem_inc(hi_out[g.index], 1)

                    does = {"Q": Q, "S": S_, "PT": PT, "OT": OT, "Y": Y, "ctx": ctx}
                    does_early = {"hT": hT}

                    def early(b):
                        for s in early_first():
                            if s[0] in does_early:
                                does_early[s[0]](b, s)

                    def main(b, steps):
                        for k, s in enumerate(steps):
                            if s[0] == "S" and steps[k + 1][0] == "PT":
                                PT(b, steps[k + 1])
                                S_(b, s)
                            elif s[0] == "PT" and steps[k - 1][0] == "S":
                                continue
                            elif s[0] in does:
                                does[s[0]](b, s)
                            elif s[0] in does_early:
                                does_early[s[0]](b + 1, s)

                    over_batches(act, early, main)

                @block.vector
                def _(dve):
                    seen = [dve.value_load(seen_flags[0:1, c:c + 1], min_val=0, max_val=1) for c in range(NCH + 1)]
                    for k in range(8):
                        dve.sem_inc(drained[k], 1)
                    dve.sem_inc(r_done, 2)
                    dve.wait_ge(presets, 4)

                    def lo_half(dst, src, scale, hi):
                        return nc.vector.scalar_tensor_tensor(out=dst, in0=src, scalar=scale, in1=hi,
                                                              op0=ALU.mult, op1=ALU.subtract)

                    def Q(b, s):
                        _, h, c = s
                        g = at[s]
                        q = slice(h * HALF, (h + 1) * HALF)
                        hi_is_out(dve, s, b)
                        nc.vector.scalar_tensor_tensor(out=qT_lo[:, c, q], in0=ps[g.index][:],
                                                       scalar=q_bias[:, c:c + 1], in1=qT_hi[:, c, q], op0=ALU.add,
                                                       op1=ALU.subtract).then_inc(drained[g.index], 1)

                    def R(b, s):
                        g = at[s]
                        is_full(dve, s, b)
                        nc.vector.tensor_scalar(r_all[:], ps[g.index][:, 0:QT], S_A * S_CTX / S_W, r_bias[:],
                                                ALU.mult, ALU.add).then_inc(drained[g.index], 1)

                    def S_(b, s):
                        t = s[1]

                        def masked(c, w):
                            g = at[s + (c,)]
                            return nc.vector.scalar_tensor_tensor(
                                out=prob[t % 2][:, cols(c)], in0=unseen[:, t, cols(c)], scalar=MASKED,
                                in1=ps[g.index][:, 0:w], op0=ALU.mult, op1=ALU.add)

                        def largest(c):
                            is_drained(dve, s + (c,), b)
                            return nc.vector.tensor_reduce(cmax[t % 2][:, c:c + 1], prob[t % 2][:, cols(c)],
                                                           AX.X, ALU.max)

                        def taken(c):
                            is_full(dve, s + (c,), b)
                            masked(c, CW).then_inc(drained[at[s + (c,)].index], 1)
                            largest(c)

                        def passed(c):
                            is_full(dve, s + (c,), b)
                            dve.sem_inc(drained[at[s + (c,)].index], 1)

                        over_chunks(dve, seen, taken, passed)
                        is_full(dve, s + (NCH,), b)
                        masked(NCH, TW).then_inc(drained[at[s + (NCH,)].index], 1)
                        largest(NCH).then_inc(chunk_max, 1)
                        dve.wait_ge(chunk_max, turn(b, t))
                        nc.vector.tensor_reduce(rmax[t % 2][:], cmax[t % 2][:], AX.X, ALU.max).then_inc(row_max, 1)
                        dve.wait_ge(row_max, turn(b, t))
                        if t == 0:
                            is_drained(dve, ("R",), b)
                        nc.vector.tensor_scalar(smax[t % 2][:], rmax[t % 2][:], FLOOR, r_all[:, t:t + 1], ALU.max,
                                                ALU.add).then_inc(held_max, 1)
                        dve.wait_ge(held_max, turn(b, t))
                        nc.vector.tensor_scalar(shift[t % 2][:], smax[t % 2][:], r_all[:, t:t + 1], -K_EXP, ALU.subtract,
                                                ALU.mult).then_inc(shift_ready, 1)

                    def PT(b, s):
                        t = s[1]
                        q = slice(t * P, (t + 1) * P)

                        def taken(c):
                            g = at[s + (c,)]
                            hi_is_out(dve, s + (c,), b)
                            lo_half(pT_lo[:, c * CB:(c + 1) * CB, q],
                                    ps[g.index][:, 0:CW].rearrange("p (j q) -> p j q", j=CB), S_P,
                                    pT_hi[:, c * CB:(c + 1) * CB, q]).then_inc(drained[g.index], 1)

                        def passed(c):
                            hi_is_out(dve, s + (c,), b)
                            dve.sem_inc(drained[at[s + (c,)].index], 1)

                        over_chunks(dve, seen, taken, passed)
                        g = at[s + (NCH,)]
                        hi_is_out(dve, s + (NCH,), b)
                        lo_half(pT_lo[0:TW, TAIL, q], ps[g.index][0:TW, 0:P], S_P,
                                pT_hi[0:TW, TAIL, q]).then_inc(drained[g.index], 1)
                        nc.vector.tensor_reduce(rsum[t % 2][:], csum[t % 2][:], AX.X, ALU.add).then_inc(row_sum, 1)
                        dve.wait_ge(row_sum, turn(b, t))
                        nc.vector.reciprocal(rinv[t % 2][:], rsum[t % 2][:]).then_inc(row_inv, 1)
                        dve.wait_ge(row_inv, turn(b, t))
                        nc.vector.tensor_scalar(o_scale[:, t:t + 1], rinv[t % 2][:], tanh_x[:], None,
                                                ALU.mult).then_inc(scale_ready, 1)

                    def OT(b, s):
                        _, h, c = s
                        g = at[s]
                        q = slice(h * HALF, (h + 1) * HALF)
                        hi_is_out(dve, s, b)
                        lo_half(qT_lo[:, c, q], ps[g.index][:], S_OUT / (S_P * S_CTX),
                                qT_hi[:, c, q]).then_inc(drained[g.index], 1)

                    def O(b, s):
                        t = s[1]
                        g = at[s]
                        xr = x_res[t % 4]
                        is_full(dve, s, b)
                        dve.wait_ge(xbias_ready, turn(b, t))
                        dve.wait_ge(scale_ready, turn(b, t))
                        nc.vector.scalar_tensor_tensor(out=xr[:], in0=ps[g.index][:], scalar=o_scale[:, t:t + 1],
                                                       in1=xr[:], op0=ALU.mult,
                                                       op1=ALU.add).then_inc(drained[g.index], 1)
                        is_drained(dve, s, b)
                        nc.vector.bn_stats(st2[t % 4][:], xr[:]).then_inc(ln2_stats, 1)
                        wait_apart(dve, ln2_stats, turn(b, t), waits_passed)
                        nc.vector.bn_aggr(mv2[t % 4][:], st2[t % 4][:]).then_inc(ln2_moments, 1)

                    def Y(b, s):
                        t = s[1]
                        dve.wait_ge(h2_ready, turn(b, t))
                        if t > 0:
                            dve.wait_ge(r_done, turn(b, t - 1) + 2)
                        nc.vector.scalar_tensor_tensor(out=junk[:], in0=h2[t % 2][:], scalar=1.0, in1=router_row[:],
                                                       op0=ALU.mult, op1=ALU.mult,
                                                       accum_out=router8[:, t:t + 1]).then_inc(r_done, 1)
                        if t == QT - 1:
                            dve.wait_ge(r_done, turn(b, t) + 2)
                            nc.vector.tensor_copy(router[:, bass.ds(b * QT, QT)], router8[:]).then_inc(r_kept, 1)

                    def stats(b, s):
                        t = s[1]
                        dve.wait_ge(x_loaded[t % 2], 16 * (QT // 2 * b + t // 2 + 1))
                        nc.vector.bn_stats(st1[t % 2][:], x_in[t % 2][:]).then_inc(ln1_stats, 1)
                        wait_apart(dve, ln1_stats, turn(b, t), waits_passed)
                        nc.vector.bn_aggr(mv1[t % 2][:], st1[t % 2][:]).then_inc(ln1_moments, 1)

                    def norm(b, s):
                        t = s[1]
                        dve.wait_ge(ln1_rstd, turn(b, t))
                        nc.vector.tensor_scalar(x_in[t % 2][:], x_in[t % 2][:], mv1[t % 2][:, 0:1], rs1[t % 2][:],
                                                ALU.subtract, ALU.mult).then_inc(h_ready, 1)

                    def hT(b, s):
                        t = s[1]
                        g = at[s]
                        q = slice(t * P, (t + 1) * P)
                        hi_is_out(dve, s, b)
                        lo_half(hT_lo[:, :, q], ps[g.index][:].rearrange("p (c q) -> p c q", c=DC), S_LN,
                                hT_hi[:, :, q]).then_inc(drained[g.index], 1)

                    def ctx(b, s):
                        j = s[1]
                        g = at[s]
                        w = P if j < TAIL else TW

                        def arrived():
                            dve.wait_ge(c_loaded[j % 4], 16 * (c_uses[j % 4] * b + j // 4 + 1))
                            hi_is_out(dve, s, b)

                        def split():
                            arrived()
                            lo_half(cT_lo[:, :, j * P:j * P + w],
                                    ps[g.index][:].rearrange("p (c k) -> p c k", c=DC)[:, :, 0:w], S_CTX,
                                    cT_hi[:, :, j * P:j * P + w]).then_inc(drained[g.index], 1)
                            lo_half(c_lo[0:w, j, :], c_in[j % 4][0:w, :], S_CTX,
                                    c_hi[0:w, j, :]).then_inc(c_used[j % 4], 1)
                        if j == TAIL:
                            split()
                        else:
                            with dve.If(seen[j // CB] > 0):
                                split()
                            with dve.Else():
                                arrived()
                                dve.sem_inc(drained[g.index], 1)
                                dve.sem_inc(c_used[j % 4], 1)

                    does = {"Q": Q, "R": R, "S": S_, "PT": PT, "OT": OT, "O": O, "Y": Y, "ctx": ctx}
                    does_early = {"stats": stats, "norm": norm, "hT": hT}

                    def early(b):
                        for s in early_first():
                            does_early[s[0]](b, s)

                    def main(b, steps):
                        for s in steps:
                            if s[0] in does:
                                does[s[0]](b, s)
                            else:
                                does_early[s[0]](b + 1, s)

                    over_batches(dve, early, main)

        with ExitStack() as part:
            def sb(name, shape, dt):
                return part.enter_context(nc.sbuf_tensor(name, shape, dt))

            def psem(name):
                return part.enter_context(nc.semaphore(name))

            NW1 = DC * (F // D)
            NW = NW1 + FT
            NSLOT = 8
            w_in = [sb(f"w_in{s}", [P, D], F32) for s in range(NSLOT)]
            w1_hi = sb("w1_hi", [P, DC, F], F16)
            w1_lo = sb("w1_lo", [P, DC, F], F16)
            w2_hi = sb("w2_hi", [P, FT, D], F16)
            w2_lo = sb("w2_lo", [P, FT, D], F16)
            b1_col = sb("b1_col", [P, FT], F32)
            b2_row = sb("b2_row", [P, D], F32)
            weight = sb("weight", [P, B * QT], F32)
            e_neg = sb("e_neg", [P, B * QT], F32)
            e_one = sb("e_one", [P, B * QT], F32)
            sig = sb("sig", [P, B * QT], F32)
            below = sb("below", [P, P], F32)
            tok_iota = sb("tok_iota", [P, QT], F32)
            slot_base = sb("slot_base", [P, 1], F32)
            row_base = sb("row_base", [P, 1], F32)
            r8 = sb("r8", [P, QT], F32)
            r_line = sb("r_line", [P, S], F32)
            cmp_junk = [sb(f"cmp_junk{s}", [P, S + P], F16) for s in range(2)]
            counts = sb("counts", [P, QT, 3], F32)
            rank = sb("rank", [P, QT], F32)
            far = sb("far", [P, QT], F32)
            slot_f = sb("slot_f", [P, QT], F32)
            slot = sb("slot", [P, QT], U32)
            entry = sb("entry", [P, QT, 2], F32)
            picked = sb("picked", [P, ST, 2], F32)
            row_next = sb("row_next", [P, ST], U32)
            row_now = sb("row_now", [P, ST], U32)
            weight_next = sb("weight_next", [P, ST], F32)
            weight_now = sb("weight_now", [P, ST], F32)
            sel = [sb(f"sel{s}", [P, D], F32) for s in range(ST)]
            selT_hi = sb("selT_hi", [P, DC, TOP], F16)
            selT_lo = sb("selT_lo", [P, DC, TOP], F16)
            act_f = [sb(f"act_f{s}", [P, TOP], F32) for s in range(2)]
            act_hi = [sb(f"act_hi{s}", [P, TOP], F16) for s in range(3)]
            act_lo = [sb(f"act_lo{s}", [P, TOP], F16) for s in range(3)]
            upd = [sb(f"upd{s}", [P, D], F32) for s in range(ST)]

            full = {k: psem(f"ffn_full{k}") for k in range(8)}
            hi_out = {k: psem(f"ffn_hi_out{k}") for k in range(8)}
            drained = {k: psem(f"ffn_drained{k}") for k in range(8)}
            w_loaded = [psem(f"w_loaded{s}") for s in range(NSLOT)]
            w_hi_done = psem("w_hi_done")
            w_lo_done = psem("w_lo_done")
            small_loaded = psem("small_loaded")
            const_ready = psem("const_ready")
            sig_step = psem("sig_step")
            weight_ready = psem("weight_ready")
            r8_ready = psem("r8_ready")
            counted = psem("counted")
            ranked = psem("ranked")
            far_ready = psem("far_ready")
            slotf_ready = psem("slotf_ready")
            entry_ready = psem("entry_ready")
            slots_ready = psem("slots_ready")
            table_written = psem("table_written")
            table_loaded = psem("table_loaded")
            rows_ready = psem("rows_ready")
            gathered = psem("gathered")
            act_hi_done = psem("act_hi_done")
            act_ready = psem("act_ready")
            upd_ready = psem("upd_ready")
            upd_added = psem("upd_added")
            adds_done = psem("adds_done")
            bases = psem("bases")

            def ffn_steps(prepare):
                steps = [("selT", s) for s in range(ST)]
                extra = {}
                if prepare:
                    extra = {1: [("line", 0), ("line", 1)], FT - 4: [("pick",)]}
                    for t in range(QT):
                        extra.setdefault(2 + t, []).append(("rank", t))
                    extra[1 + QT] = extra[1 + QT] + [("slots",)]
                for f in range(FT + 2):
                    if f < FT:
                        steps.append(("up", f))
                    if f == 0:
                        steps.append(("now",))
                    if f >= 2:
                        steps.append(("down", f - 2))
                    steps += extra.get(f, [])
                return steps + [("upd", s) for s in range(ST)]

            at = share_banks([s for s in ffn_steps(False) if s[0] in ("selT", "up")], [0, 1, 2],
                             lambda s: s[0] == "selT")
            at.update(share_banks([("line", 0), ("line", 1)], [7], lambda s: False))
            at.update({("upd", s): Bank(3 + s, 1, 1, 0, 0) for s in range(ST)})

            def is_drained(eng, step, b):
                g = at[step]
                eng.wait_ge(drained[g.index], g.use(b) + 1)

            def is_full(eng, step, b):
                g = at[step]
                eng.wait_ge(full[g.index], g.use(b))

            def is_free(eng, step, b):
                g = at[step]
                eng.wait_ge(drained[g.index], g.use(b))

            def hi_is_out(eng, step, b):
                g = at[step]
                eng.wait_ge(hi_out[g.index], g.split(b))

            def over_batches(eng, main):
                with eng.Fori(0, B - 1) as b:
                    main(b, ffn_steps(True))
                main(B - 1, ffn_steps(False))

            with nc.Block() as block:
                @block.sync
                def _(sp):
                    sp.dma_start(b2_row[:], b2.partition_broadcast(P)).then_inc(small_loaded, 16)
                    with nc.allow_non_contiguous_dma(reason="two thousand bias values, once"):
                        sp.dma_start(b1_col[:], b1.rearrange("(f p) -> p f", p=P)).then_inc(small_loaded, 16)
                    for n in range(NW):
                        if n < NW1:
                            src = W1[(n % DC) * P:(n % DC + 1) * P, (n // DC) * D:(n // DC + 1) * D]
                        else:
                            src = W2[(n - NW1) * P:(n - NW1 + 1) * P, :]
                        if n >= NSLOT:
                            sp.wait_ge(w_lo_done, n - NSLOT + 1)
                        sp.dma_start(w_in[n % NSLOT][:], src).then_inc(w_loaded[n % NSLOT], 16)

                    def pick(b):
                        sp.wait_ge(table_written, 16 * QT * (b + 1))
                        sp.dma_start(picked[:], slot_table[bass.ds(b * TOP, TOP), :]
                                     .rearrange("(s p) c -> p s c", p=P)).then_inc(table_loaded, 16)

                    pick(0)
                    with sp.Fori(0, B - 1) as b:
                        pick(b + 1)

                @block.gpsimd
                def _(pool):
                    nc.gpsimd.memset(below[:], 1.0).then_inc(const_ready, 1)
                    pool.wait_ge(const_ready, 1)
                    nc.gpsimd.affine_select(out=below[:], in_=below[:], compare_op=ALU.is_ge, fill=0.0, base=-1,
                                            pattern=[[-1, P]], channel_multiplier=1).then_inc(const_ready, 1)
                    nc.gpsimd.iota(tok_iota[:], [[P, QT]], base=0, channel_multiplier=1,
                                   allow_small_or_imprecise_dtypes=True).then_inc(const_ready, 1)
                    nc.gpsimd.memset(slot_base[:], 0.0).then_inc(const_ready, 1)
                    nc.gpsimd.memset(row_base[:], 0.0).then_inc(const_ready, 1)
                    nc.gpsimd.memset(counts[:], 0.0).then_inc(const_ready, 1)
                    pool.sem_inc(adds_done, 1)

                    def fill_table(b):
                        wait_apart(pool, entry_ready, b + 1, waits_passed)
                        wait_apart(pool, slots_ready, b + 1, waits_passed)
                        for t in range(QT):
                            pool.indirect_dma_start(slot_table, bass.IndirectOffsetOnAxis(ap=slot[:, t:t + 1], axis=0),
                                                    entry[:, t, :], None, bounds_check=B * TOP - 1,
                                                    oob_is_err=False).then_inc(table_written, 16)

                    def gather(b):
                        wait_apart(pool, rows_ready, b + 1, waits_passed)
                        for s in range(ST):
                            pool.indirect_dma_start(sel[s][:], None, h2_rows,
                                                    bass.IndirectOffsetOnAxis(ap=row_next[:, s:s + 1], axis=0),
                                                    bounds_check=B * S - 1,
                                                    oob_is_err=True).then_inc(gathered, 16)

                    def main(b, steps):
                        for s in steps:
                            if s[0] == "slots":
                                fill_table(b + 1)
                            if s[0] == "pick":
                                gather(b + 1)
                            if s[0] == "upd":
                                k = s[1]
                                wait_apart(pool, upd_ready, ST * b + k + 1, waits_passed)
                                pool.indirect_dma_start(out_rows,
                                                        bass.IndirectOffsetOnAxis(ap=row_now[:, k:k + 1], axis=0),
                                                        upd[k][:], None, bounds_check=B * S - 1, oob_is_err=True,
                                                        compute_op=ALU.add).then_inc(upd_added, 16)
                        pool.wait_ge(upd_added, 16 * ST * (b + 1))
                        pool.sem_inc(adds_done, 1)

                    fill_table(0)
                    gather(0)
                    over_batches(pool, main)
                    pool.wait_ge(upd_added, 16 * ST * B)

                @block.tensor
                def _(pe):
                    def line(b, s):
                        g = at[s]
                        pe.wait_ge(r8_ready, b + 1)
                        is_free(pe, s, b)
                        for k in range(4):
                            t = 4 * s[1] + k
                            last = pe.transpose(ps[g.index][:, k * P:(k + 1) * P],
                                                r8[:, t:t + 1].to_broadcast([P, P]), ident[:])
                        last.then_inc(full[g.index], 1)

                    def selT(b, s):
                        k = s[1]
                        g = at[s]
                        if k == 0:
                            pe.wait_ge(gathered, 16 * ST * (b + 1))
                        is_free(pe, s, b)
                        for d in range(DC):
                            last = pe.transpose(ps[g.index][:, d * P:(d + 1) * P], sel[k][:, d * P:(d + 1) * P],
                                                ident[:])
                        last.then_inc(full[g.index], 1)

                    def up(b, s):
                        f = s[1]
                        g = at[s]
                        if f == 0:
                            is_drained(pe, ("selT", ST - 1), b)
                        is_free(pe, s, b)
                        pe.wait_ge(w_lo_done, DC * (f * P // D + 1))
                        fs = slice(f * P, (f + 1) * P)
                        for d in range(DC):
                            for k, (st, mo) in enumerate(((w1_hi, selT_hi), (w1_hi, selT_lo), (w1_lo, selT_hi))):
                                last = pe.matmul(ps[g.index][:], st[:, d, fs], mo[:, d, :],
                                                 start=(d == 0 and k == 0), stop=(d == DC - 1 and k == 2))
                        last.then_inc(full[g.index], 1)

                    def down(b, s):
                        f = s[1]
                        pe.wait_ge(act_ready, FT * b + f + 3)
                        pe.wait_ge(w_lo_done, NW1 + f + 1)
                        for k in range(ST):
                            g = at[("upd", k)]
                            if f == 0:
                                is_free(pe, ("upd", k), b)
                            ts = slice(k * P, (k + 1) * P)
                            for n, (st, mo) in enumerate(((act_hi, w2_hi), (act_hi, w2_lo), (act_lo, w2_hi))):
                                last = pe.matmul(ps[g.index][:], st[f % 3][:, ts], mo[:, f, :],
                                                 start=(f == 0 and n == 0), stop=(f == FT - 1 and n == 2),
                                                 skip_group_check=True)
                            if f == FT - 1:
                                last.then_inc(full[g.index], 1)

                    def main(b, steps):
                        for s in steps:
                            if s[0] == "line":
                                line(b + 1, s)
                            elif s[0] in ("selT", "up", "down"):
                                {"selT": selT, "up": up, "down": down}[s[0]](b, s)

                    line(0, ("line", 0))
                    line(0, ("line", 1))
                    over_batches(pe, main)

                @block.scalar
                def _(act):
                    nc.scalar.activation(e_neg[:], router[:], ACT.Exp, scale=-1.0).then_inc(sig_step, 1)
                    for n in range(NW):
                        act.wait_ge(w_loaded[n % NSLOT], 16 * (n // NSLOT + 1))
                        dst = w1_hi[:, n % DC, (n // DC) * D:(n // DC + 1) * D] if n < NW1 else w2_hi[:, n - NW1, :]
                        nc.scalar.activation(dst, w_in[n % NSLOT][:], ACT.Copy, scale=S_W).then_inc(w_hi_done, 1)
                    act.wait_ge(small_loaded, 32)

                    def main(b, steps):
                        for s in steps:
                            if s[0] == "selT":
                                g = at[s]
                                is_full(act, s, b)
                                nc.scalar.activation(selT_hi[:, :, s[1] * P:(s[1] + 1) * P],
                                                     ps[g.index][:].rearrange("p (c q) -> p c q", c=DC),
                                                     ACT.Copy, scale=S_LN).then_inc(hi_out[g.index], 1)
                            if s[0] == "up":
                                f = s[1]
                                g = at[s]
                                is_full(act, s, b)
                                act.wait_ge(act_ready, FT * b + f + 1)
                                nc.scalar.activation(act_f[f % 2][:], ps[g.index][:], ACT.Gelu_apprx_tanh,
                                                     bias=b1_col[:, f:f + 1],
                                                     scale=1.0 / (S_LN * S_W)).then_inc(drained[g.index], 1)
                                is_drained(act, s, b)
                                nc.scalar.activation(act_hi[f % 3][:], act_f[f % 2][:], ACT.Copy,
                                                     scale=S_G).then_inc(act_hi_done, 1)

                    over_batches(act, main)

                @block.vector
                def _(dve):
                    for k in range(8):
                        dve.sem_inc(drained[k], 1)
                    dve.sem_inc(act_ready, 2)

                    def take_scores(b):
                        if not isinstance(b, int) or b > 0:
                            dve.wait_ge(table_written, 16 * QT * b)
                        nc.vector.tensor_copy(r8[:], router[:, bass.ds(b * QT, QT)]).then_inc(r8_ready, 1)
                        nc.vector.tensor_scalar(entry[:, :, 0], tok_iota[:], row_base[:], None,
                                                ALU.add)
                        nc.vector.tensor_copy(entry[:, :, 1], weight[:, bass.ds(b * QT, QT)]).then_inc(entry_ready, 1)
                        nc.vector.tensor_scalar(row_base[:], row_base[:], float(S), None, ALU.add).then_inc(bases, 1)

                    def line(b, s):
                        g = at[s]
                        is_full(dve, s, b)
                        nc.vector.tensor_copy(r_line[:, s[1] * BANK:(s[1] + 1) * BANK],
                                              ps[g.index][:]).then_inc(drained[g.index], 1)
                        is_drained(dve, s, b)

                    def rank_tile(b, s):
                        t = s[1]
                        me = r8[:, t:t + 1]
                        junk = cmp_junk[t % 2]
                        if t > 1:
                            dve.wait_ge(counted, QT * b + t - 1)
                        if t > 0:
                            nc.vector.tensor_scalar(junk[:, 0:t * P], r_line[:, 0:t * P], me, None, ALU.is_ge,
                                                    ALU.add, accum_out=counts[:, t, 0:1])
                        nc.vector.tensor_scalar(junk[:, t * P:S], r_line[:, t * P:S], me, None, ALU.is_gt,
                                                ALU.add, accum_out=counts[:, t, 1:2])
                        nc.vector.scalar_tensor_tensor(out=junk[:, S:S + P], in0=r_line[:, t * P:(t + 1) * P],
                                                       scalar=me, in1=below[:], op0=ALU.is_equal, op1=ALU.mult,
                                                       accum_out=counts[:, t, 2:3]).then_inc(counted, 1)

                    def slots(b):
                        dve.wait_ge(counted, QT * (b + 1))
                        nc.vector.tensor_reduce(rank[:], counts[:], AX.X, ALU.add).then_inc(ranked, 1)
                        dve.wait_ge(ranked, b + 1)
                        nc.vector.tensor_scalar(far[:], rank[:], float(TOP), FAR, ALU.is_ge,
                                                ALU.mult).then_inc(far_ready, 1)
                        dve.wait_ge(far_ready, b + 1)
                        nc.vector.scalar_tensor_tensor(out=slot_f[:], in0=rank[:], scalar=slot_base[:], in1=far[:],
                                                       op0=ALU.add, op1=ALU.add).then_inc(slotf_ready, 1)
                        dve.wait_ge(slotf_ready, b + 1)
                        nc.vector.tensor_copy(slot[:], slot_f[:]).then_inc(slots_ready, 1)
                        nc.vector.tensor_scalar(slot_base[:], slot_base[:], float(TOP), None,
                                                ALU.add).then_inc(bases, 1)

                    def pick(b):
                        dve.wait_ge(table_loaded, 16 * (b + 1))
                        nc.vector.tensor_copy(weight_next[:], picked[:, :, 1])
                        nc.vector.tensor_copy(row_next[:], picked[:, :, 0]).then_inc(rows_ready, 1)

                    dve.wait_ge(const_ready, 6)
                    dve.wait_ge(sig_step, 1)
                    nc.vector.tensor_scalar(e_one[:], e_neg[:], 1.0, None, ALU.add).then_inc(sig_step, 1)
                    dve.wait_ge(sig_step, 2)
                    nc.vector.reciprocal(sig[:], e_one[:]).then_inc(sig_step, 1)
                    dve.wait_ge(sig_step, 3)
                    nc.vector.tensor_scalar(weight[:], sig[:], tanh_f[:], None, ALU.mult).then_inc(weight_ready, 1)
                    dve.wait_ge(weight_ready, 1)
                    take_scores(0)
                    line(0, ("line", 0))
                    line(0, ("line", 1))
                    for n in range(NW):
                        if n < QT:
                            rank_tile(0, ("rank", n))
                        if n == QT:
                            slots(0)
                        dve.wait_ge(w_hi_done, n + 1)
                        if n < NW1:
                            c, q = n % DC, slice((n // DC) * D, (n // DC + 1) * D)
                            lo, hi = w1_lo[:, c, q], w1_hi[:, c, q]
                        else:
                            lo, hi = w2_lo[:, n - NW1, :], w2_hi[:, n - NW1, :]
                        nc.vector.scalar_tensor_tensor(out=lo, in0=w_in[n % NSLOT][:], scalar=S_W, in1=hi, op0=ALU.mult,
                                                       op1=ALU.subtract).then_inc(w_lo_done, 1)
                    pick(0)
                    dve.wait_ge(small_loaded, 32)

                    def main(b, steps):
                        for s in steps:
                            if s[0] == "selT":
                                g = at[s]
                                q = slice(s[1] * P, (s[1] + 1) * P)
                                hi_is_out(dve, s, b)
                                nc.vector.scalar_tensor_tensor(
                                    out=selT_lo[:, :, q], in0=ps[g.index][:].rearrange("p (c q) -> p c q", c=DC),
                                    scalar=S_LN, in1=selT_hi[:, :, q], op0=ALU.mult,
                                    op1=ALU.subtract).then_inc(drained[g.index], 1)
                            elif s[0] == "now":
                                dve.wait_ge(adds_done, b + 1)
                                nc.vector.tensor_copy(row_now[:], row_next[:])
                                nc.vector.tensor_copy(weight_now[:], weight_next[:])
                                if ("line", 0) in steps:
                                    take_scores(b + 1)
                            elif s[0] == "up":
                                f = s[1]
                                dve.wait_ge(act_hi_done, FT * b + f + 1)
                                nc.vector.scalar_tensor_tensor(out=act_lo[f % 3][:], in0=act_f[f % 2][:], scalar=S_G,
                                                               in1=act_hi[f % 3][:], op0=ALU.mult,
                                                               op1=ALU.subtract).then_inc(act_ready, 1)
                            elif s[0] == "line":
                                line(b + 1, s)
                            elif s[0] == "rank":
                                rank_tile(b + 1, s)
                            elif s[0] == "slots":
                                slots(b + 1)
                            elif s[0] == "pick":
                                pick(b + 1)
                            elif s[0] == "upd":
                                k = s[1]
                                g = at[s]
                                is_full(dve, s, b)
                                nc.vector.scalar_tensor_tensor(out=upd[k][:], in0=ps[g.index][:],
                                                               scalar=1.0 / (S_G * S_W), in1=b2_row[:], op0=ALU.mult,
                                                               op1=ALU.add).then_inc(drained[g.index], 1)
                                is_drained(dve, s, b)
                                nc.vector.tensor_scalar(upd[k][:], upd[k][:], weight_now[:, k:k + 1], None,
                                                        ALU.mult).then_inc(upd_ready, 1)

                    over_batches(dve, main)


_INS = ['x', 'ctx_1024', 'mask_SxS2_bk0', 'g_xattn', 'g_ffn', 'L0_xattn_Wq', 'L0_xattn_bq', 'L0_xattn_Wk',
        'L0_xattn_bk', 'L0_xattn_Wv', 'L0_xattn_bv', 'L0_ffn_w_router', 'L0_ffn_W1', 'L0_ffn_b1', 'L0_ffn_W2',
        'L0_ffn_b2']
_OUTS = [((8, 1024, 512), 'float32')]


def kernel(**inputs):
    import numpy as _np
    import concourse.bacc as _bacc
    from concourse import mybir as _mybir
    from concourse.bass_utils import run_bass_kernel_spmd as _run

    nc = _bacc.Bacc("TRN2", target_bir_lowering=False, num_devices=1)
    arrays, args = {}, []
    for name in _INS:
        a = _np.ascontiguousarray(inputs[name])
        arrays[f"in_{name}_dram"] = a
        args.append(nc.dram_tensor(f"in_{name}_dram", a.shape, _mybir.dt.from_np(a.dtype), kind="ExternalInput").ap())
    for i, (shape, dtype) in enumerate(_OUTS):
        dt = _mybir.dt.from_np(_np.dtype(dtype))
        args.append(nc.dram_tensor(f"out_{i}_dram", shape, dt, kind="ExternalOutput").ap())
    flamingo_gated_layer(nc, *args)
    r = _run(nc, [arrays], core_ids=[0])
    return r.results[0]["out_0_dram"]
```
